# Optimizing a Trainium2 kernel written in Bass

```python
import numpy as np
import jax
import jax.numpy as jnp

def _softmax(x, axis=-1):
    return jax.nn.softmax(x, axis=axis)

def _gelu(x):
    return jax.nn.gelu(x, approximate=True)

def _silu(x):
    return jax.nn.silu(x)

def _sigmoid(x):
    return jax.nn.sigmoid(x)

def _layernorm(x, axis=-1, eps=1e-05):
    m = jnp.mean(x, axis=axis, keepdims=True)
    v = jnp.var(x, axis=axis, keepdims=True)
    return (x - m) / jnp.sqrt(v + eps)

def _scatter_add(tgt, idx, src, axis=0):
    return tgt.at[idx].add(src)

def _segment_sum(src, seg, n):
    return jax.ops.segment_sum(src, seg, n)
kernel_name = 'mk_vit_tower_cls_d1_tok_img1024_r4_543267'

def setup_inputs(seed: int=0):
    np.random.seed(seed)
    _w = jnp.asarray

    def _rec_inputs():
        import jax
        import jax.numpy as jnp
        _rk = jax.random.key(seed)
        x = -0.00016672 + 0.999947 * jax.random.normal(jax.random.fold_in(_rk, 1), (32, 3, 96, 96), jnp.float32)
        cls_tok = 0.02 * jax.random.normal(jax.random.fold_in(_rk, 5), (1, 1, 256), jnp.float32)
        return (x, cls_tok)
    x, cls_tok = _rec_inputs()

    def _L0_tok_setup():
        import jax, jax.numpy as jnp
        import numpy as np
        DIM = 256
        IMG = 96
        P = 16
        C = 3
        TEMP = 10000.0
        EPS = 1e-05
        PATCH_DIM = C * P * P
        HP = IMG // P

        def layernorm(x, gamma, beta):
            mu = jnp.mean(x, axis=-1, keepdims=True)
            var = jnp.var(x, axis=-1, keepdims=True)
            return (x - mu) * jax.lax.rsqrt(var + EPS) * gamma + beta

        def posemb_sincos_2d(h, w, dim, dtype):
            y, x = jnp.meshgrid(jnp.arange(h), jnp.arange(w), indexing='ij')
            omega = jnp.arange(dim // 4, dtype=jnp.float32) / (dim // 4 - 1)
            omega = 1.0 / TEMP ** omega
            y = y.reshape(-1)[:, None] * omega[None, :]
            x = x.reshape(-1)[:, None] * omega[None, :]
            pe = jnp.concatenate((jnp.sin(x), jnp.cos(x), jnp.sin(y), jnp.cos(y)), axis=1)
            return pe.astype(dtype)
        key = jax.random.key(seed)
        ks = jax.random.split(key, 8)
        B = 64
        img = jax.random.normal(ks[0], (B, C, IMG, IMG), dtype=jnp.float32)
        cls_token = jax.random.normal(ks[1], (1, 1, DIM), dtype=jnp.float32)
        cls_pos_embedding = jax.random.normal(ks[2], (1, 1, DIM), dtype=jnp.float32)
        ln1_g = jnp.ones((PATCH_DIM,), jnp.float32)
        ln1_b = jnp.zeros((PATCH_DIM,), jnp.float32)
        W = jax.random.normal(ks[3], (PATCH_DIM, DIM), dtype=jnp.float32) / np.sqrt(PATCH_DIM)
        bias = jnp.zeros((DIM,), jnp.float32)
        ln2_g = jnp.ones((DIM,), jnp.float32)
        ln2_b = jnp.zeros((DIM,), jnp.float32)
        return {'img': img, 'cls_token': cls_token, 'cls_pos_embedding': cls_pos_embedding, 'ln1_g': ln1_g, 'ln1_b': ln1_b, 'W': W, 'bias': bias, 'ln2_g': ln2_g, 'ln2_b': ln2_b}
    _L0_tok_all = _L0_tok_setup()
    _L0_tok_in = {k: v for k, v in _L0_tok_all.items() if k in ('cls_token', 'cls_pos_embedding', 'ln1_g', 'ln1_b', 'W', 'bias', 'ln2_g', 'ln2_b')}
    del _L0_tok_all

    def _L0_attn_setup():
        import jax, jax.numpy as jnp
        import numpy as np
        import math
        N_EMBD = 256
        N_HEAD = 16
        N_LAYER = 12
        key = jax.random.key(seed)
        kx, kw, kb = jax.random.split(key, 3)
        B, T, C = (4, 512, N_EMBD)
        x = jax.random.normal(kx, (B, T, C), dtype=jnp.float32)
        bound = 1.0 / math.sqrt(C)
        W = jax.random.uniform(kw, (3 * C, C), minval=-bound, maxval=bound, dtype=jnp.float32)
        W = W * (1.0 / math.sqrt(N_LAYER * 2))
        b = jax.random.uniform(kb, (3 * C,), minval=-bound, maxval=bound, dtype=jnp.float32)
        return {'x': x, 'W': W, 'b': b}
    _L0_attn_all = _L0_attn_setup()
    _L0_attn_in = {k: v for k, v in _L0_attn_all.items() if k in ('W', 'b')}
    del _L0_attn_all

    def _L0_ffn_setup():
        import jax, jax.numpy as jnp
        import numpy as np
        E, D, F = (8, 256, 1024)
        B, S = (4, 512)

        def _layernorm(x, g, b, eps=1e-05):
            mu = jnp.mean(x, axis=-1, keepdims=True)
            var = jnp.var(x, axis=-1, keepdims=True)
            return (x - mu) * jax.lax.rsqrt(var + eps) * g + b
        key = jax.random.key(seed)
        ks = jax.random.split(key, 5)
        return {'input_features': jax.random.normal(ks[0], (B, S, D), jnp.float32), 'centroids': jax.random.normal(ks[1], (E, D), jnp.float32) * 0.1, 'ln_g': jnp.ones((E, D), jnp.float32), 'ln_b': jnp.zeros((E, D), jnp.float32), 'w1': jax.random.normal(ks[2], (E, F, D), jnp.float32) * (1.0 / np.sqrt(D).astype(np.float32)), 'b1': jnp.zeros((E, F), jnp.float32), 'w2': jax.random.normal(ks[3], (E, D, F), jnp.float32) * (1.0 / np.sqrt(F).astype(np.float32)), 'b2': jnp.zeros((E, D), jnp.float32)}
    _L0_ffn_all = _L0_ffn_setup()
    _L0_ffn_in = {k: v for k, v in _L0_ffn_all.items() if k in ('centroids', 'ln_g', 'ln_b', 'w1', 'b1', 'w2', 'b2')}
    del _L0_ffn_all
    return {'x': x, 'cls_tok': cls_tok, 'L0_tok_cls_token': _L0_tok_in['cls_token'], 'L0_tok_cls_pos_embedding': _L0_tok_in['cls_pos_embedding'], 'L0_tok_ln1_g': _L0_tok_in['ln1_g'], 'L0_tok_ln1_b': _L0_tok_in['ln1_b'], 'L0_tok_W': _L0_tok_in['W'], 'L0_tok_bias': _L0_tok_in['bias'], 'L0_tok_ln2_g': _L0_tok_in['ln2_g'], 'L0_tok_ln2_b': _L0_tok_in['ln2_b'], 'L0_attn_W': _L0_attn_in['W'], 'L0_attn_b': _L0_attn_in['b'], 'L0_ffn_centroids': _L0_ffn_in['centroids'], 'L0_ffn_ln_g': _L0_ffn_in['ln_g'], 'L0_ffn_ln_b': _L0_ffn_in['ln_b'], 'L0_ffn_w1': _L0_ffn_in['w1'], 'L0_ffn_b1': _L0_ffn_in['b1'], 'L0_ffn_w2': _L0_ffn_in['w2'], 'L0_ffn_b2': _L0_ffn_in['b2']}

def reference(x, cls_tok, L0_tok_cls_token, L0_tok_cls_pos_embedding, L0_tok_ln1_g, L0_tok_ln1_b, L0_tok_W, L0_tok_bias, L0_tok_ln2_g, L0_tok_ln2_b, L0_attn_W, L0_attn_b, L0_ffn_centroids, L0_ffn_ln_g, L0_ffn_ln_b, L0_ffn_w1, L0_ffn_b1, L0_ffn_w2, L0_ffn_b2):
    import jax
    import jax.numpy as jnp

    def _L0_tok_ref(img, cls_token, cls_pos_embedding, ln1_g, ln1_b, W, bias, ln2_g, ln2_b):
        import jax, jax.numpy as jnp
        import numpy as np
        DIM = 256
        IMG = 96
        P = 16
        C = 3
        TEMP = 10000.0
        EPS = 1e-05
        PATCH_DIM = C * P * P
        HP = IMG // P

        def layernorm(x, gamma, beta):
            mu = jnp.mean(x, axis=-1, keepdims=True)
            var = jnp.var(x, axis=-1, keepdims=True)
            return (x - mu) * jax.lax.rsqrt(var + EPS) * gamma + beta

        def posemb_sincos_2d(h, w, dim, dtype):
            y, x = jnp.meshgrid(jnp.arange(h), jnp.arange(w), indexing='ij')
            omega = jnp.arange(dim // 4, dtype=jnp.float32) / (dim // 4 - 1)
            omega = 1.0 / TEMP ** omega
            y = y.reshape(-1)[:, None] * omega[None, :]
            x = x.reshape(-1)[:, None] * omega[None, :]
            pe = jnp.concatenate((jnp.sin(x), jnp.cos(x), jnp.sin(y), jnp.cos(y)), axis=1)
            return pe.astype(dtype)
        b = img.shape[0]
        x = img.reshape(b, C, HP, P, HP, P)
        x = jnp.transpose(x, (0, 2, 4, 3, 5, 1))
        x = x.reshape(b, HP, HP, PATCH_DIM)
        x = layernorm(x, ln1_g, ln1_b)
        x = jnp.einsum('bhwp,pd->bhwd', x, W) + bias
        x = layernorm(x, ln2_g, ln2_b)
        pe = posemb_sincos_2d(HP, HP, DIM, x.dtype)
        x = x.reshape(b, HP * HP, DIM) + pe[None]
        cls_tokens = jnp.broadcast_to(cls_token + cls_pos_embedding, (b, 1, DIM))
        return jnp.concatenate((cls_tokens, x), axis=1)

    def _L0_attn_ref(x, W, b):
        import jax, jax.numpy as jnp
        import numpy as np
        import math
        N_EMBD = 256
        N_HEAD = 16
        N_LAYER = 12
        B, T, C = x.shape
        H = N_HEAD
        D = C // H
        qkv = jnp.einsum('btc,oc->bto', x, W) + b
        q, k, v = jnp.split(qkv, 3, axis=-1)
        q = q.reshape(B, T, H, D).transpose(0, 2, 1, 3)
        k = k.reshape(B, T, H, D).transpose(0, 2, 1, 3)
        v = v.reshape(B, T, H, D).transpose(0, 2, 1, 3)
        att = jnp.einsum('bhtd,bhsd->bhts', q, k) / math.sqrt(D)
        causal = jnp.tril(jnp.ones((T, T), dtype=bool))
        att = jnp.where(causal, att, -jnp.inf)
        att = jax.nn.softmax(att, axis=-1)
        y = jnp.einsum('bhts,bhsd->bhtd', att, v)
        return y.transpose(0, 2, 1, 3).reshape(B, T, C)

    def _L0_ffn_ref(input_features, centroids, ln_g, ln_b, w1, b1, w2, b2):
        import jax, jax.numpy as jnp
        import numpy as np
        E, D, F = (8, 256, 1024)
        B, S = (4, 512)

        def _layernorm(x, g, b, eps=1e-05):
            mu = jnp.mean(x, axis=-1, keepdims=True)
            var = jnp.var(x, axis=-1, keepdims=True)
            return (x - mu) * jax.lax.rsqrt(var + eps) * g + b
        Bf, Sf, Df = input_features.shape
        x = input_features.reshape(-1, Df)
        aff = x @ centroids.T
        assign = jnp.argmax(aff, axis=1)
        order = jnp.argsort(assign)
        xs = x[order]
        es = assign[order]
        alpha = jax.nn.sigmoid(jnp.take_along_axis(aff[order], es[:, None], axis=1))
        nE = centroids.shape[0]
        y = jnp.zeros_like(xs)
        for e in range(nE):
            h = _layernorm(xs, ln_g[e], ln_b[e])
            h = jax.nn.relu(h @ w1[e].T + b1[e])
            ye = xs + h @ w2[e].T + b2[e]
            y = y + jnp.where((es == e)[:, None], ye, 0.0)
        out_sorted = alpha * y + (1.0 - alpha) * xs
        inv = jnp.argsort(order)
        return out_sorted[inv].reshape(Bf, Sf, Df)
    h = _L0_tok_ref(x, L0_tok_cls_token, L0_tok_cls_pos_embedding, L0_tok_ln1_g, L0_tok_ln1_b, L0_tok_W, L0_tok_bias, L0_tok_ln2_g, L0_tok_ln2_b)
    h = jnp.concatenate([jnp.broadcast_to(cls_tok, (h.shape[0], 1, h.shape[2])), h], axis=1)
    h = h + _L0_attn_ref(_layernorm(h, axis=-1), L0_attn_W, L0_attn_b)
    h = h + _L0_ffn_ref(_layernorm(h, axis=-1), L0_ffn_centroids, L0_ffn_ln_g, L0_ffn_ln_b, L0_ffn_w1, L0_ffn_b1, L0_ffn_w2, L0_ffn_b2)
    return h

_drawn_inputs = setup_inputs


def setup_inputs(seed=0):
    import zlib

    import numpy as np

    out = dict(_drawn_inputs(seed))
    spreads = {'L0_tok_ln1_g': (1.0, 0.2),
     'L0_tok_ln1_b': (0.0, 0.1),
     'L0_tok_bias': (0.0, 0.1),
     'L0_tok_ln2_g': (1.0, 0.2),
     'L0_tok_ln2_b': (0.0, 0.1),
     'L0_ffn_ln_g': (1.0, 0.2),
     'L0_ffn_ln_b': (0.0, 0.294),
     'L0_ffn_b1': (0.0, 0.288),
     'L0_ffn_b2': (0.0, 0.1)}
    factors = {}
    for name, (base, spread) in spreads.items():
        noise = np.random.default_rng([zlib.crc32(name.encode()), seed]).standard_normal(out[name].shape)
        drawn = base * np.exp(spread * noise) if base else spread * noise
        out[name] = jnp.asarray(drawn.astype(out[name].dtype))
    for name, factor in factors.items():
        out[name] = (out[name] * factor).astype(out[name].dtype)
    return out
```

```python
from contextlib import ExitStack

import numpy as np

import concourse.bass as bass
from concourse import mybir

F32 = mybir.dt.float32
I32 = mybir.dt.int32
ALU = mybir.AluOpType
ACT = mybir.ActivationFunctionType
AX = mybir.AxisListType

IMAGES, CHANNELS, SIDE, PATCH = 32, 3, 96, 16
GRID = SIDE // PATCH
PATCHES = GRID * GRID
PATCH_DIM = CHANNELS * PATCH * PATCH
D = 256
HEADS, HEAD_DIM = 16, 16
EXPERTS, HIDDEN = 8, 1024
EPS = 1e-5
TEMPERATURE = 10000.0
P = 128

T = PATCHES + 2
PER_TILE = 3
TT = PER_TILE * T
TP = PER_TILE * PATCHES
TILES = -(-IMAGES // PER_TILE)
LAST_IMAGES = IMAGES - (TILES - 1) * PER_TILE
TOKENS = IMAGES * T
KX = PATCH_DIM // P
KD = D // P
KF = HIDDEN // P
HC = P // HEAD_DIM
GROUPS = -(-HEADS // PER_TILE)
VW = HEAD_DIM + 1
MASKED = -1e30

SLOT_TILES = (TOKENS - EXPERTS) // P + EXPERTS
ROW = 2 * D + 8
NO_TOKEN = 4096.0
RING = 3

_WIDTHS = [("ident", P), ("before", P), ("iota", P), ("head_of_row", HC), ("head_in_stack", HEADS),
           ("causal", T), ("token", TILES), ("live", TILES), ("ge_slots", SLOT_TILES - 1),
           ("gt_slots", TOKENS // P + 1), ("tile_no", SLOT_TILES), ("rank", EXPERTS),
           ("restart", EXPERTS * TILES)]
COLS = {}
_at = 0
for _name, _width in _WIDTHS:
    COLS[_name] = (_at, _width)
    _at += _width
TABLE = _at


def attention_tower(nc, x, tok_add, tok_add2, tok_gain, ln1_g, ln1_b, tok_w, tok_bias, wqk, wv, bqk, bv,
                    centroids, expert_cols, expert_b2, w1, w2, table, out):
    rows_dram = nc.dram_tensor("token_rows", (TOKENS, ROW), F32)
    with ExitStack() as ctx:
        def sb(name, shape, dt=F32):
            return ctx.enter_context(nc.sbuf_tensor(name, shape, dt))

        def sem(name):
            return ctx.enter_context(nc.semaphore(name))

        tab = sb("tab", [P, TABLE])
        ones = sb("ones", [P, P])
        w1_sb = sb("w1_sb", [P, EXPERTS, KD, HIDDEN])
        w2_sb = sb("w2_sb", [P, EXPERTS, KF, D])
        b2_sb = sb("b2_sb", [P, EXPERTS, D])
        cols_sb = sb("cols_sb", [P, EXPERTS, 2 * KD + KF])
        cent_sb = sb("cent_sb", [P, KD, EXPERTS])
        aff_all = sb("aff_all", [P, TILES, EXPERTS])

        phase_a = ExitStack()

        def sa(name, shape, dt=F32):
            return phase_a.enter_context(nc.sbuf_tensor(name, shape, dt))

        tokw = sa("tokw", [P, KX, D])
        tok_row = sa("tok_row", [TT, D])
        gain = sa("gain", [TT, D])
        shift = sa("shift", [TT, D])
        ln1 = sa("ln1", [P, 2, KX])
        wqk_sb = sa("wqk_sb", [P, KD, 2 * D])
        wv_sb = sa("wv_sb", [P, KD, D])
        bqk_sb = sa("bqk_sb", [P, 4])
        bv_sb = sa("bv_sb", [TT, D])
        xin = sa("xin", [TP, 2, PATCH_DIM])
        xT = sa("xT", [P, KX, TT])
        z = sa("z", [TT, D])
        h = sa("h", [TT, D])
        hb = sa("hb", [TT, 2, D])
        hn = sa("hn", [TT, D])
        hT = sa("hT", [P, KD, PER_TILE, PER_TILE, T])
        qT = sa("qT", [P, KD, PER_TILE * (TT + T)])
        kT = sa("kT", [P, KD, TT])
        kblk = sa("kblk", [P, KD, PER_TILE, HC, T])
        vblk = sa("vblk", [TT, PER_TILE, HEADS, VW])
        ln1_bcast = kblk[:, :, :, :, :].rearrange("p c i a k -> p (c i a k)")[:, 0:KX * TT]\
            .rearrange("p (c n) -> p c n", c=KX)
        prob = sa("prob", [TT, HEADS, T])
        probT = sa("probT", [TT, GROUPS, PER_TILE * (TT + T)])
        h1 = sa("h1", [TT, D])
        shift2 = h1
        xn = sa("xn", [TT, D])
        xnT = sa("xnT", [P, KD, TT])
        stats = sa("stats", [TT, 5, 2, 6])
        mv = sa("mv", [TT, 5, 2])
        eps_col = sa("eps_col", [TT, 1])
        half_col = sa("half_col", [TT, 1])
        var_eps = sa("var_eps", [TT, 5])
        rstd = sa("rstd", [TT, 5])
        smax = sa("smax", [TT, HEADS])
        srec = sa("srec", [TT, HEADS])
        amax = sa("amax", [TT, 1])
        aexp = sa("aexp", [TT, 1])
        ainc = sa("ainc", [TT, 1])
        rowbuf = sa("rowbuf", [TT, 2, ROW])
        phase_a.close()

        onehot = sb("onehot", [P, EXPERTS, TILES])
        r_max = sb("r_max", [P, TILES])
        r_val = sb("r_val", [P, TILES, EXPERTS])
        r_first = sb("r_first", [P, TILES])
        through = sb("through", [P, EXPERTS, TILES])
        tot = sb("tot", [P, EXPERTS, TILES])
        r_cmp = sb("r_cmp", [P, EXPERTS, TOKENS // P + 1])
        n_tiles = sb("n_tiles", [P, EXPERTS])
        tile_end = sb("tile_end", [P, EXPERTS])
        tile_start = sb("tile_start", [P, EXPERTS])
        place = sb("place", [P, EXPERTS, TILES])
        pos = sb("pos", [P, TILES])
        r_ge = sb("r_ge", [P, TILES, SLOT_TILES - 1])
        slot_tile = sb("slot_tile", [P, TILES])
        slot_row = sb("slot_row", [P, TILES])
        tile_hot = sb("tile_hot", [P, TILES, SLOT_TILES])
        row_hot = sb("row_hot", [P, TILES, P])
        slot = sb("slot", [P, SLOT_TILES])
        slot_m1 = sb("slot_m1", [P, SLOT_TILES])
        empty = sb("empty", [P, SLOT_TILES])
        gather_all = sb("gather_all", [P, SLOT_TILES], I32)
        scatter_all = sb("scatter_all", [P, SLOT_TILES], I32)
        e_cmp = sb("e_cmp", [P, SLOT_TILES, EXPERTS])
        e_sum = sb("e_sum", [P, SLOT_TILES])
        expert = sb("expert", [P, SLOT_TILES], I32)

        gather_idx = sb("gather_idx", [P, RING], I32)
        scatter_idx = sb("scatter_idx", [P, RING], I32)
        cur = sb("cur", [P, RING, 2 * KD + KF])
        rows = sb("rows", [P, RING, ROW])
        zT = sb("zT", [P, KD, P])
        hid = sb("hid", [P, HIDDEN])
        hidT = sb("hidT", [P, KF, P])
        y1 = sb("y1", [P, D])
        yout = sb("yout", [P, RING, D])

        ps = ctx.enter_context(nc.psum_tensor("ps", [P, 8, 512], F32))

        def c(name, n=P):
            a, w = COLS[name]
            return tab[0:n, a:a + w]

        ident = c("ident")

        def bank(n, width, parts=P, banks=1):
            return ps[0:parts, n:n + banks, :].rearrange("p b n -> p (b n)")[:, 0:width]

        p_xT = ps[:, 0:2, 0:3 * TP]
        p_v = bank(0, PER_TILE * D, TT, 2)
        p_z = bank(2, D, TT)
        p_hT = bank(3, KD * TT)
        p_aff = ps[0:TT, 2, 256:256 + EXPERTS]
        p_qk = bank(4, 4 * TT)
        p_o = bank(5, HEADS * VW, TT)
        p_s = ps[0:TT, 6:8, 0:HC * T]
        p_pT = [ps[0:TT, 6, 0:4 * TT], ps[0:TT, 7, 0:2 * TT]]
        p_count = bank(2, 2 * EXPERTS * TILES)
        p_slot = bank(4, SLOT_TILES)
        p_zT = bank(0, KD * P)
        p_up = bank(1, HIDDEN, P, 2)
        p_hidT = bank(5, KF * P, P, 2)
        p_down = bank(7, D)

        s_consts = sem("consts_loaded")
        s_w = sem("experts_loaded")
        s_set = sem("buffers_set")
        s_wfold = sem("tok_weights_scaled")
        s_lnb = sem("ln1_shift_spread")
        s_crow_ps = sem("tok_row_summed")
        s_crow = sem("tok_row_ready")
        s_shift = sem("shift_ready")
        s_x = [sem("x_loaded_even"), sem("x_loaded_odd")]
        s_xstat = sem("x_stats")
        s_xmv = sem("x_moments")
        s_xn = sem("x_normalised")
        s_xTp = sem("x_transposed")
        s_xT = sem("xT_ready")
        s_zp = sem("z_summed")
        s_z = sem("z_ready")
        s_zstat = sem("z_stats")
        s_zmv = sem("z_moments")
        s_zn = sem("z_normalised")
        s_zg = sem("z_scaled")
        s_h = sem("h_ready")
        s_hstat = sem("h_stats")
        s_hmv = sem("h_moments")
        s_hn = sem("h_normalised")
        s_hb = sem("h_plus_bv")
        s_hTp = sem("h_transposed")
        s_hT = sem("hT_ready")
        s_qkp = sem("qk_projected")
        s_q = sem("q_ready")
        s_k = sem("k_ready")
        s_kblk = sem("k_blocks_ready")
        s_vp = sem("v_projected")
        s_v = sem("v_blocks_ready")
        s_sp = sem("scores_summed")
        s_sm = sem("scores_masked")
        s_smax = sem("score_max")
        s_sub = sem("scores_shifted")
        s_exp = sem("exp_done")
        s_pTp = sem("probs_transposed")
        s_pT = sem("probT_ready")
        s_o = sem("attention_summed")
        s_rec = sem("sums_inverted")
        s_on = sem("attention_scaled")
        s_h1 = sem("h1_ready")
        s_h1stat = sem("h1_stats")
        s_h1mv = sem("h1_moments")
        s_x2 = sem("xn_ready")
        s_base = sem("base_ready")
        s_x2stat = sem("xn_stats")
        s_x2mv = sem("xn_moments")
        s_row = sem("row_zn_ready")
        s_xnTp = sem("xn_transposed")
        s_xnT = sem("xnT_ready")
        s_affp = sem("affinity_summed")
        s_aff = sem("affinity_kept")
        s_amax = sem("affinity_max")
        s_aexp = sem("alpha_exp")
        s_ainc = sem("alpha_plus_one")
        s_alpha = sem("alpha_ready")
        s_stored = [sem("rows_stored_even"), sem("rows_stored_odd")]
        s_var = [sem(f"variance_eps_{n}") for n in range(5)]
        s_rstd = [sem(f"rstd_{n}") for n in range(5)]

        s_passed_dve = sem("waits_passed_vector")
        s_passed_pool = sem("waits_passed_pool")
        SETS = 5 + 3 + PER_TILE
        CONSTS = 16 * 15
        LN_X, LN_Z, LN_H, LN_H1, LN_XN = range(5)

        def in_loop(t):
            return not isinstance(t, int)

        def above_zero(count):
            return in_loop(count) or count > 0

        def lacks(t, ahead):
            return not in_loop(t) and not 0 <= t + ahead < TILES

        def last(t):
            return not in_loop(t) and t == TILES - 1

        PAIRS = (1, (TILES - 3) // 2)
        SLOT_RINGS = (1, (SLOT_TILES - RING) // RING)

        r_dve = sem("routing_step")
        s_hot = sem("onehot_ready")
        s_count = sem("counts_summed")
        s_rowhot = sem("slot_hots_ready")
        s_slotp = sem("slots_summed")
        s_route = sem("routing_ready")
        s_idx = sem("index_columns_ready")
        s_gather = [sem(f"rows_gathered_{n}") for n in range(RING)]
        s_scatter = [sem(f"rows_scattered_{n}") for n in range(RING)]
        s_cur = sem("expert_columns_ready")
        s_zTp = sem("zn_transposed")
        s_zTe = sem("zT_ready")
        s_up = sem("up_summed")
        s_hid = sem("hidden_kept")
        s_hidTp = sem("hidden_transposed")
        s_relu = sem("hidden_relu")
        s_down = sem("down_summed")
        s_y1 = sem("y_plus_b2")
        s_y = sem("y_ready")

        block = ctx.enter_context(nc.Block())

        @block.sync
        def _(sp):
            def load_x(j, b):
                t = 2 * j + b
                if above_zero(t - 1):
                    sp.wait_ge(s_xTp, t - 1)
                n = LAST_IMAGES * PATCHES if last(t) else TP
                sp.dma_start(xin[0:n, b, :], x[bass.ds(t * TP, n), :]).then_inc(s_x[b], 16)

            def load_expert(e):
                sp.dma_start(w1_sb[:, bass.ds(e, 1), :, :].rearrange("p e c n -> p (e c n)"),
                             w1[bass.ds(e * P, P), :]).then_inc(s_w, 16)
                sp.dma_start(w2_sb[:, bass.ds(e, 1), :, :].rearrange("p e c n -> p (e c n)"),
                             w2[bass.ds(e * P, P), :]).then_inc(s_w, 16)

            def store_rows(j, b):
                t = 2 * j + b
                sp.wait_ge(s_row, t + 1)
                sp.wait_ge(s_base, t + 1)
                sp.wait_ge(s_alpha, t + 1)
                n = LAST_IMAGES * T if last(t) else TT
                sp.dma_start(rows_dram[bass.ds(t * TT, n), :], rowbuf[0:n, b, :]).then_inc(s_stored[b], 16)

            def step(j, b):
                t = 2 * j + b
                if not lacks(t, 2):
                    load_x(j + 1, b)
                if in_loop(t) or t < EXPERTS:
                    load_expert(t)
                if not lacks(t, -1):
                    store_rows(j - 1 + b, 1 - b)

            load_x(0, 0)
            load_x(0, 1)
            step(0, 0)
            step(0, 1)
            with sp.Fori(*PAIRS) as j:
                step(j, 0)
                step(j, 1)
            for t in range(TILES - 3, TILES):
                step(t // 2, t % 2)
            store_rows((TILES - 1) // 2, (TILES - 1) % 2)

        @block.gpsimd
        def _(pool):
            def inv_std(n, moments, t, parts=TT):
                pool.wait_ge(moments, t + 1)
                nc.gpsimd.tensor_tensor(var_eps[0:parts, n:n + 1], mv[0:parts, n, 1:2], eps_col[0:parts, :],
                                        ALU.add).then_inc(s_var[n], 1)
                pool.wait_ge(s_var[n], t + 1)
                nc.gpsimd.tensor_tensor(rstd[0:parts, n:n + 1], var_eps[0:parts, n:n + 1], half_col[0:parts, :],
                                        ALU.pow).then_inc(s_rstd[n], 1)

            def key_blocks(t):
                pool.wait_ge(s_k, t + 1)
                if above_zero(t):
                    pool.wait_ge(s_sp, t)
                for ch in range(KD):
                    for i in range(PER_TILE):
                        ins = nc.gpsimd.tensor_tensor(
                            kblk[:, ch, i, :, :],
                            kT[:, ch, i * T:(i + 1) * T].unsqueeze(1).to_broadcast([P, HC, T]),
                            c("head_of_row").unsqueeze(2).to_broadcast([P, HC, T]), ALU.mult)
                ins.then_inc(s_kblk, 1)

            def base(j, b):
                t = 2 * j + b
                pool.wait_ge(s_x2, t + 1)
                if above_zero(16 * j):
                    pool.wait_ge(s_stored[b], 16 * j)
                nc.gpsimd.tensor_tensor(rowbuf[:, b, D:2 * D], h1[:, :], xn[:, :], ALU.add).then_inc(s_base, 1)

            def value_bias(t, b):
                pool.wait_ge(s_h, t + 1)
                if above_zero(t - 1):
                    pool.wait_ge(s_h1, t - 1)
                nc.gpsimd.tensor_tensor(hb[:, b, :], h[:, :], bv_sb[:, :], ALU.add).then_inc(s_hb, 1)

            nc.gpsimd.memset(eps_col[:], EPS).then_inc(s_set, 1)
            nc.gpsimd.memset(half_col[:], -0.5).then_inc(s_set, 1)
            nc.gpsimd.memset(xT[:], 0.0).then_inc(s_set, 1)
            nc.gpsimd.memset(qT[:], 0.0).then_inc(s_set, 1)
            nc.gpsimd.memset(probT[:], 0.0).then_inc(s_set, 1)
            pool.wait_ge(s_set, SETS)
            pool.wait_ge(s_consts, CONSTS)

            inv_std(LN_X, s_xmv, 0, TP)
            inv_std(LN_Z, s_zmv, 0)
            value_bias(0, 0)
            inv_std(LN_H, s_hmv, 0)
            inv_std(LN_X, s_xmv, 1, TP)

            def step(j, b):
                t = 2 * j + b
                key_blocks(t)
                if not lacks(t, -1):
                    inv_std(LN_H1, s_h1mv, t - 1)
                if not lacks(t, 1):
                    inv_std(LN_Z, s_zmv, t + 1)
                if not lacks(t, -1):
                    inv_std(LN_XN, s_x2mv, t - 1)
                    base(j - 1 + b, 1 - b)
                if not lacks(t, 1):
                    value_bias(t + 1, 1 - b)
                    inv_std(LN_H, s_hmv, t + 1)
                if not lacks(t, 2):
                    inv_std(LN_X, s_xmv, t + 2, TP)

            step(0, 0)
            step(0, 1)
            with pool.Fori(*PAIRS) as j:
                step(j, 0)
                step(j, 1)
            for t in range(TILES - 3, TILES):
                step(t // 2, t % 2)
            inv_std(LN_H1, s_h1mv, TILES - 1)
            inv_std(LN_XN, s_x2mv, TILES - 1)
            base((TILES - 1) // 2, (TILES - 1) % 2)

            pool.wait_ge(s_stored[0], 16 * -(-TILES // 2))
            pool.wait_ge(s_stored[1], 16 * (TILES // 2))

            def gather(j, u):
                t = RING * j + u
                pool.wait_ge(s_idx, t + 1)
                if above_zero(t - RING + 1):
                    pool.wait_ge(s_y, t - RING + 1)
                pool.sem_inc(s_passed_pool, 1)
                nc.gpsimd.indirect_dma_start(
                    rows[:, u, :], None, rows_dram[:, :],
                    bass.IndirectOffsetOnAxis(ap=gather_idx[:, u:u + 1], axis=0)).then_inc(s_gather[u], 16)

            def scatter(j, u):
                t = RING * j + u
                pool.wait_ge(s_y, t + 1)
                pool.sem_inc(s_passed_pool, 1)
                nc.gpsimd.indirect_dma_start(
                    out, bass.IndirectOffsetOnAxis(ap=scatter_idx[:, u:u + 1], axis=0), yout[:, u, :], None,
                    bounds_check=TOKENS - 1, oob_is_err=False).then_inc(s_scatter[u], 16)

            def slot_step(j, u):
                scatter(j, u)
                t = RING * j + u
                if in_loop(t) or t + RING < SLOT_TILES:
                    gather(j + 1, u)

            for u in range(RING):
                gather(0, u)
            for u in range(RING):
                slot_step(0, u)
            with pool.Fori(*SLOT_RINGS) as j:
                for u in range(RING):
                    slot_step(j, u)
            for t in range(SLOT_RINGS[1] * RING, SLOT_TILES):
                slot_step(t // RING, t % RING)
            for u in range(RING):
                pool.wait_ge(s_scatter[u], 16 * len(range(u, SLOT_TILES, RING)))

        @block.scalar
        def _(act):
            small = [(tab[:, :], table), (ln1[:, 0, :], ln1_g), (ln1[:, 1, :], ln1_b),
                     (tokw[:, :, :].rearrange("p c n -> p (c n)"), tok_w), (tok_row[:, :], tok_bias.partition_broadcast(TT)),
                     (gain[:, :], tok_gain), (shift[:, :], tok_add), (shift2[:, :], tok_add2),
                     (wqk_sb[:, :, :].rearrange("p c n -> p (c n)"), wqk), (bqk_sb[:, :], bqk),
                     (wv_sb[:, :, :].rearrange("p c n -> p (c n)"), wv), (bv_sb[:, :], bv.partition_broadcast(TT)),
                     (cent_sb[:, :, :].rearrange("p c n -> p (c n)"), centroids),
                     (cols_sb[:, :, :].rearrange("p e n -> p (e n)"), expert_cols),
                     (b2_sb[:, :, :].rearrange("p e n -> p (e n)"), expert_b2.partition_broadcast(P))]
            assert CONSTS == 16 * len(small)
            for to, source in small:
                act.dma_start(to, source).then_inc(s_consts, 16)

            def x_out(t):
                act.wait_ge(s_xTp, t + 1)
                if above_zero(t):
                    act.wait_ge(s_zp, t)
                for g in range(2):
                    ins = nc.scalar.activation(
                        xT[:, 3 * g:3 * g + 3, :].rearrange("p c (i k) -> p c i k", i=PER_TILE)[:, :, :, 2:T],
                        p_xT[:, g, :].rearrange("p (c i k) -> p c i k", c=3, i=PER_TILE), ACT.Copy)
                ins.then_inc(s_xT, 1)

            def h_out(t):
                act.wait_ge(s_hTp, t + 1)
                if above_zero(t):
                    act.wait_ge(s_vp, t)
                for k in range(KD):
                    source = p_hT[:, k * TT:(k + 1) * TT].rearrange("p (i k) -> p i k", i=PER_TILE)
                    ins = nc.scalar.activation(
                        hT[:, k], source.unsqueeze(2).to_broadcast([P, PER_TILE, PER_TILE, T]), ACT.Copy)
                ins.then_inc(s_hT, 1)

            def k_out(t):
                act.wait_ge(s_qkp, t + 1)
                if above_zero(t):
                    act.wait_ge(s_kblk, t)
                for ch in range(KD):
                    ins = nc.scalar.activation(kT[:, ch, :], p_qk[:, (KD + ch) * TT:(KD + ch + 1) * TT],
                                               ACT.Identity, bias=bqk_sb[:, KD + ch:KD + ch + 1])
                ins.then_inc(s_k, 1)

            def q_out(t):
                if above_zero(t):
                    act.wait_ge(s_sp, t)
                blocks = qT[:, :, :].rearrange("p c (i s) -> p c i s", i=PER_TILE)[:, :, :, 0:T]
                for ch in range(KD):
                    ins = nc.scalar.activation(
                        blocks[:, ch], p_qk[:, ch * TT:(ch + 1) * TT].rearrange("p (i k) -> p i k", i=PER_TILE),
                        ACT.Identity, bias=bqk_sb[:, ch:ch + 1], scale=float(HEAD_DIM) ** -0.5)
                ins.then_inc(s_q, 1)

            def exps(t):
                act.wait_ge(s_sub, t + 1)
                nc.scalar.activation(prob[:, :, :], prob[:, :, :], ACT.Exp).then_inc(s_exp, 1)

            def prob_out(t):
                act.wait_ge(s_pTp, t + 1)
                if above_zero(t):
                    act.wait_ge(s_o, t)
                blocks = probT[:, :, :].rearrange("p g (i s) -> p g i s", i=PER_TILE)[:, :, :, 0:T]
                nc.scalar.activation(blocks[:, 0:4], p_pT[0].rearrange("p (g i k) -> p g i k", g=4, i=PER_TILE), ACT.Copy)
                nc.scalar.activation(blocks[:, 4], p_pT[1][:, 0:TT].rearrange("p (i k) -> p i k", i=PER_TILE), ACT.Copy)
                nc.scalar.activation(blocks[0:T, 5], p_pT[1][0:T, TT:2 * TT].rearrange("p (i k) -> p i k", i=PER_TILE),
                                     ACT.Copy).then_inc(s_pT, 1)

            def xn_out(t):
                act.wait_ge(s_xnTp, t + 1)
                if above_zero(t):
                    act.wait_ge(s_affp, t)
                nc.scalar.activation(xnT[:, :, :].rearrange("p c n -> p (c n)"), p_hT, ACT.Copy).then_inc(s_xnT, 1)

            def alpha_exp(t):
                act.wait_ge(s_amax, t + 1)
                nc.scalar.activation(aexp[:, :], amax[:, :], ACT.Exp, scale=-1.0).then_inc(s_aexp, 1)

            act.wait_ge(s_set, SETS)
            act.wait_ge(s_consts, CONSTS)
            x_out(0)
            h_out(0)

            def step(j, b):
                t = 2 * j + b
                k_out(t)
                q_out(t)
                if not lacks(t, 1):
                    x_out(t + 1)
                exps(t)
                if not lacks(t, -1):
                    xn_out(t - 1)
                prob_out(t)
                if not lacks(t, -1):
                    alpha_exp(t - 1)
                if not lacks(t, 1):
                    h_out(t + 1)

            step(0, 0)
            step(0, 1)
            with act.Fori(*PAIRS) as j:
                step(j, 0)
                step(j, 1)
            for t in range(TILES - 3, TILES):
                step(t // 2, t % 2)
            xn_out(TILES - 1)
            alpha_exp(TILES - 1)

            def slot_step(j, u):
                t = RING * j + u
                act.wait_ge(s_hidTp, t + 1)
                act.wait_ge(s_cur, t + 1)
                if above_zero(t):
                    act.wait_ge(s_down, t)
                for k in range(KF):
                    nc.scalar.activation(hidT[:, k, :], p_hidT[:, k * P:(k + 1) * P], ACT.Relu,
                                         bias=cur[:, u, 2 * KD + k:2 * KD + k + 1]).then_inc(s_relu, 1)

            for u in range(RING):
                slot_step(0, u)
            with act.Fori(*SLOT_RINGS) as j:
                for u in range(RING):
                    slot_step(j, u)
            for t in range(SLOT_RINGS[1] * RING, SLOT_TILES):
                slot_step(t // RING, t % RING)

        @block.tensor
        def _(pe):
            def x_turn(t, b):
                pe.wait_ge(s_xn, t + 1)
                if above_zero(t - 1):
                    pe.wait_ge(s_v, t - 1)
                for k in range(KX):
                    ins = nc.tensor.transpose(p_xT[:, k // 3, (k % 3) * TP:(k % 3 + 1) * TP],
                                              xin[:, b, k * P:(k + 1) * P], ident[0:TP, 0:TP])
                ins.then_inc(s_xTp, 1)

            def embed(t):
                pe.wait_ge(s_xT, t + 1)
                if above_zero(t):
                    pe.wait_ge(s_z, t)
                if above_zero(t - 2):
                    pe.wait_ge(s_aff, t - 2)
                for k in range(KX):
                    ins = nc.tensor.matmul(p_z, xT[:, k, :], tokw[:, k, :], start=k == 0, stop=k == KX - 1)
                ins.then_inc(s_zp, 1)

            def h_turn(t):
                pe.wait_ge(s_hn, t + 1)
                if above_zero(t - 1):
                    pe.wait_ge(s_xnT, t - 1)
                for k in range(KD):
                    ins = nc.tensor.transpose(p_hT[:, k * TT:(k + 1) * TT], hn[:, k * P:(k + 1) * P], ident[0:TT, 0:TT])
                ins.then_inc(s_hTp, 1)

            def project_qk(t):
                pe.wait_ge(s_hT, t + 1)
                if above_zero(t):
                    pe.wait_ge(s_q, t)
                if above_zero(t):
                    pe.wait_ge(s_k, t)
                for m in range(2 * KD):
                    for k in range(KD):
                        ins = nc.tensor.matmul(p_qk[:, m * TT:(m + 1) * TT], wqk_sb[:, k, m * P:(m + 1) * P],
                                               hT[:, k, :, 0, :], start=k == 0, stop=k == KD - 1)
                ins.then_inc(s_qkp, 1)

            def project_v(t):
                pe.wait_ge(s_xT, t + 2 if in_loop(t) else min(t + 2, TILES))
                for i in range(PER_TILE):
                    for k in range(KD):
                        ins = nc.tensor.matmul(
                            p_v[:, i * D:(i + 1) * D],
                            hT[:, k, i, :, :].rearrange("p r k -> p (r k)"),
                            wv_sb[:, k, :], start=k == 0, stop=k == KD - 1)
                ins.then_inc(s_vp, 1)

            def scores(t):
                pe.wait_ge(s_q, t + 1)
                pe.wait_ge(s_kblk, t + 1)
                if above_zero(t):
                    pe.wait_ge(s_pT, t)
                for ch in range(KD):
                    for i in range(PER_TILE):
                        ins = nc.tensor.matmul(p_s[:, ch, :], qT[:, ch, i * TT:(i + 1) * TT],
                                               kblk[:, ch, i, :, :].rearrange("p a k -> p (a k)"),
                                               start=i == 0, stop=i == PER_TILE - 1)
                ins.then_inc(s_sp, 1)

            def prob_turn(t):
                pe.wait_ge(s_exp, t + 1)
                flat = prob[:, :, :].rearrange("p a k -> p (a k)")
                for g in range(GROUPS):
                    n = min(TT, HEADS * T - g * TT)
                    ins = nc.tensor.transpose(p_pT[g // 4][0:n, (g % 4) * TT:(g % 4 + 1) * TT],
                                              flat[:, g * TT:g * TT + n], ident[0:TT, 0:TT])
                ins.then_inc(s_pTp, 1)

            def attend(t):
                pe.wait_ge(s_pT, t + 1)
                pe.wait_ge(s_v, t + 1)
                if above_zero(t):
                    pe.wait_ge(s_on, t)
                for g in range(GROUPS):
                    heads = min(PER_TILE, HEADS - g * PER_TILE)
                    rows_g = heads * T
                    for i in range(PER_TILE):
                        ins = nc.tensor.matmul(
                            p_o[:, g * PER_TILE * VW:(g * PER_TILE + heads) * VW],
                            probT[0:rows_g, g, i * TT:(i + 1) * TT],
                            vblk[0:rows_g, i, g * PER_TILE:g * PER_TILE + heads, :].rearrange("p a v -> p (a v)"),
                            start=i == 0, stop=i == PER_TILE - 1)
                ins.then_inc(s_o, 1)

            def xn_turn(t):
                pe.wait_ge(s_x2, t + 1)
                pe.wait_ge(s_hT, t + 2 if in_loop(t) else min(t + 2, TILES))
                for k in range(KD):
                    ins = nc.tensor.transpose(p_hT[:, k * TT:(k + 1) * TT], xn[:, k * P:(k + 1) * P], ident[0:TT, 0:TT])
                ins.then_inc(s_xnTp, 1)

            def affinity(t):
                pe.wait_ge(s_xnT, t + 1)
                pe.wait_ge(s_z, t + 3 if in_loop(t) else min(t + 3, TILES))
                for k in range(KD):
                    ins = nc.tensor.matmul(p_aff, xnT[:, k, :], cent_sb[:, k, :], start=k == 0, stop=k == KD - 1)
                ins.then_inc(s_affp, 1)

            pe.wait_ge(s_set, SETS)
            pe.wait_ge(s_consts, CONSTS)
            pe.wait_ge(s_lnb, 1)
            for k in range(KX):
                ins = nc.tensor.matmul(p_z, ln1_bcast[:, k, :], tokw[:, k, :],
                                       start=k == 0, stop=k == KX - 1)
            ins.then_inc(s_crow_ps, 1)
            pe.wait_ge(s_wfold, 1)
            pe.wait_ge(s_crow, 1)
            x_turn(0, 0)
            embed(0)
            h_turn(0)

            def step(j, b):
                t = 2 * j + b
                project_qk(t)
                if not lacks(t, 1):
                    x_turn(t + 1, 1 - b)
                    embed(t + 1)
                scores(t)
                project_v(t)
                if not lacks(t, -1):
                    xn_turn(t - 1)
                prob_turn(t)
                if not lacks(t, -1):
                    affinity(t - 1)
                attend(t)
                if not lacks(t, 1):
                    h_turn(t + 1)

            step(0, 0)
            step(0, 1)
            with pe.Fori(*PAIRS) as j:
                step(j, 0)
                step(j, 1)
            for t in range(TILES - 3, TILES):
                step(t // 2, t % 2)
            xn_turn(TILES - 1)
            affinity(TILES - 1)

            ET = EXPERTS * TILES
            hot = onehot[0:TT, :, :].rearrange("p e t -> p (e t)")
            pe.wait_ge(s_hot, 1)
            nc.tensor.matmul(p_count[0:TT, 0:ET], c("before", TT)[:, 0:TT], hot, start=True, stop=True)
            nc.tensor.matmul(p_count[:, ET:2 * ET], ones[0:TT, :], hot, start=True, stop=True).then_inc(s_count, 1)
            pe.wait_ge(s_rowhot, 1)
            for t in range(TILES):
                ins = nc.tensor.matmul(p_slot, row_hot[0:TT, t, :], tile_hot[0:TT, t, :],
                                       start=t == 0, stop=t == TILES - 1)
            ins.then_inc(s_slotp, 1)

            def zn_turn(j, u):
                t = RING * j + u
                pe.wait_ge(s_gather[u], 16 * (j + 1))
                if above_zero(t):
                    pe.wait_ge(s_zTe, t)
                for k in range(KD):
                    ins = nc.tensor.transpose(p_zT[:, k * P:(k + 1) * P], rows[:, u, k * P:(k + 1) * P], ident)
                ins.then_inc(s_zTp, 1)

            def up(t):
                e = pe.value_load(expert[0:1, bass.ds(t, 1)], min_val=0, max_val=EXPERTS - 1)
                pe.wait_ge(s_zTe, t + 1)
                if above_zero(t):
                    pe.wait_ge(s_hid, t)
                for n in range(HIDDEN // 512):
                    for k in range(KD):
                        ins = nc.tensor.matmul(
                            p_up[:, n * 512:(n + 1) * 512], zT[:, k, :],
                            w1_sb[:, bass.ds(e, 1), k, n * 512:(n + 1) * 512].rearrange("p e n -> p (e n)"),
                            start=k == 0, stop=k == KD - 1)
                ins.then_inc(s_up, 1)

            def hidden_turn(t):
                pe.wait_ge(s_hid, t + 1)
                if above_zero(KF * t):
                    pe.wait_ge(s_relu, KF * t)
                for k in range(KF):
                    ins = nc.tensor.transpose(p_hidT[:, k * P:(k + 1) * P], hid[:, k * P:(k + 1) * P], ident)
                ins.then_inc(s_hidTp, 1)

            def down(t):
                e = pe.value_load(expert[0:1, bass.ds(t, 1)], min_val=0, max_val=EXPERTS - 1)
                if above_zero(t):
                    pe.wait_ge(s_y1, t)
                for k in range(KF):
                    pe.wait_ge(s_relu, KF * t + k + 1)
                    ins = nc.tensor.matmul(p_down, hidT[:, k, :],
                                           w2_sb[:, bass.ds(e, 1), k, :].rearrange("p e n -> p (e n)"),
                                           start=k == 0, stop=k == KF - 1)
                ins.then_inc(s_down, 1)

            pe.wait_ge(s_w, 16 * 2 * EXPERTS)
            pe.wait_ge(s_route, 1)
            zn_turn(0, 0)
            up(0)
            zn_turn(0, 1)

            def slot_step(j, u):
                t = RING * j + u
                hidden_turn(t)
                if in_loop(t) or t + 1 < SLOT_TILES:
                    up(t + 1)
                if in_loop(t) or t + 2 < SLOT_TILES:
                    zn_turn(j + (u + 2) // RING, (u + 2) % RING)
                down(t)

            for u in range(RING):
                slot_step(0, u)
            with pe.Fori(*SLOT_RINGS) as j:
                for u in range(RING):
                    slot_step(j, u)
            for t in range(SLOT_RINGS[1] * RING, SLOT_TILES):
                slot_step(t // RING, t % RING)

        @block.vector
        def _(dve):
            def moments(n, ready, s_stat, s_mv, t, pieces, parts=TT):
                for i, piece in enumerate(pieces):
                    ins = nc.vector.bn_stats(stats[0:parts, n, i, :], piece)
                ins.then_inc(s_stat, 1)
                dve.wait_ge(s_stat, t + 1)
                dve.sem_inc(s_passed_dve, 1)
                nc.vector.bn_aggr(mv[0:parts, n, :],
                                  stats[0:parts, n, 0:len(pieces), :].rearrange("p a s -> p (a s)")).then_inc(s_mv, 1)

            def normalise(to, source, n, t, parts=TT):
                dve.wait_ge(s_rstd[n], t + 1)
                return nc.vector.tensor_scalar(to, source, mv[0:parts, n, 0:1], rstd[0:parts, n:n + 1],
                                               ALU.subtract, ALU.mult)

            def x_moments(j, b):
                t = 2 * j + b
                dve.wait_ge(s_x[b], 16 * (j + 1))
                half = PATCH_DIM // 2
                moments(LN_X, None, s_xstat, s_xmv, t, [xin[:, b, 0:half], xin[:, b, half:PATCH_DIM]], TP)

            def x_norm(t, b):
                normalise(xin[:, b, :], xin[:, b, :], LN_X, t, TP).then_inc(s_xn, 1)

            def z_moments(t):
                dve.wait_ge(s_zp, t + 1)
                nc.vector.tensor_tensor(z[:, :], p_z, tok_row[:, :], ALU.add).then_inc(s_z, 1)
                dve.wait_ge(s_z, t + 1)
                moments(LN_Z, None, s_zstat, s_zmv, t, [z[:, :]])

            def h_moments(t):
                normalise(z[:, :], z[:, :], LN_Z, t).then_inc(s_zn, 1)
                dve.wait_ge(s_zn, t + 1)
                nc.vector.tensor_tensor(z[:, :], z[:, :], gain[:, :], ALU.mult).then_inc(s_zg, 1)
                dve.wait_ge(s_zg, t + 1)
                if above_zero(t):
                    dve.wait_ge(s_hb, t)
                nc.vector.tensor_tensor(h[:, :], z[:, :], shift[:, :], ALU.add).then_inc(s_h, 1)
                dve.wait_ge(s_h, t + 1)
                moments(LN_H, None, s_hstat, s_hmv, t, [h[:, :]])

            def h_norm(t):
                if above_zero(t):
                    dve.wait_ge(s_hTp, t)
                normalise(hn[:, :], h[:, :], LN_H, t).then_inc(s_hn, 1)

            def v_out(t):
                dve.wait_ge(s_vp, t + 1)
                if above_zero(t):
                    dve.wait_ge(s_o, t)
                nc.vector.tensor_tensor(
                    vblk[:, :, :, 0:HEAD_DIM], p_v.rearrange("p (i a d) -> p i a d", i=PER_TILE, a=HEADS),
                    c("head_in_stack", TT).unsqueeze(1).unsqueeze(3).to_broadcast([TT, PER_TILE, HEADS, HEAD_DIM]),
                    ALU.mult).then_inc(s_v, 1)

            def softmax_in(t):
                dve.wait_ge(s_sp, t + 1)
                if above_zero(t):
                    dve.wait_ge(s_pTp, t)
                nc.vector.tensor_tensor(
                    prob[:, :, :].rearrange("p (c a) k -> p c a k", c=KD), p_s.rearrange("p c (a k) -> p c a k", a=HC),
                    c("causal", TT).unsqueeze(1).unsqueeze(1).to_broadcast([TT, KD, HC, T]), ALU.add).then_inc(s_sm, 1)
                dve.wait_ge(s_sm, t + 1)
                nc.vector.tensor_reduce(smax[:, :], prob[:, :, :], AX.X, ALU.max).then_inc(s_smax, 1)
                dve.wait_ge(s_smax, t + 1)
                nc.vector.tensor_tensor(prob[:, :, :], prob[:, :, :],
                                        smax[:, :].unsqueeze(2).to_broadcast([TT, HEADS, T]),
                                        ALU.subtract).then_inc(s_sub, 1)

            def h1_moments(t, b):
                dve.wait_ge(s_o, t + 1)
                o = p_o.rearrange("p (a v) -> p a v", a=HEADS)
                nc.vector.reciprocal(srec[:, :], o[:, :, HEAD_DIM]).then_inc(s_rec, 1)
                dve.wait_ge(s_rec, t + 1)
                if above_zero(t):
                    dve.wait_ge(s_base, t)
                nc.vector.tensor_tensor(h1[:, :].rearrange("p (a d) -> p a d", a=HEADS), o[:, :, 0:HEAD_DIM],
                                        srec[:, :].unsqueeze(2).to_broadcast([TT, HEADS, HEAD_DIM]),
                                        ALU.mult).then_inc(s_on, 1)
                dve.wait_ge(s_on, t + 1)
                dve.wait_ge(s_hb, t + 1)
                nc.vector.tensor_tensor(h1[:, :], h1[:, :], hb[:, b, :], ALU.add).then_inc(s_h1, 1)
                dve.wait_ge(s_h1, t + 1)
                moments(LN_H1, None, s_h1stat, s_h1mv, t, [h1[:, :]])

            def xn_moments(t):
                if above_zero(t):
                    dve.wait_ge(s_xnTp, t)
                if above_zero(t):
                    dve.wait_ge(s_base, t)
                normalise(xn[:, :], h1[:, :], LN_H1, t).then_inc(s_x2, 1)
                dve.wait_ge(s_x2, t + 1)
                moments(LN_XN, None, s_x2stat, s_x2mv, t, [xn[:, :]])

            def zn_row(j, b):
                t = 2 * j + b
                if above_zero(16 * j):
                    dve.wait_ge(s_stored[b], 16 * j)
                normalise(rowbuf[:, b, 0:D], xn[:, :], LN_XN, t).then_inc(s_row, 1)

            def keep_affinity(t):
                dve.wait_ge(s_affp, t + 1)
                nc.vector.tensor_copy(aff_all[0:TT, bass.ds(t, 1), :].rearrange("p t e -> p (t e)"), p_aff)\
                    .then_inc(s_aff, 1)
                dve.wait_ge(s_aff, t + 1)
                if above_zero(t):
                    dve.wait_ge(s_aexp, t)
                dve.sem_inc(s_passed_dve, 1)
                nc.vector.tensor_reduce(amax[:, :], aff_all[0:TT, bass.ds(t, 1), :].rearrange("p t e -> p (t e)"),
                                        AX.X, ALU.max).then_inc(s_amax, 1)

            def alpha(t, b):
                dve.wait_ge(s_aexp, t + 1)
                nc.vector.tensor_scalar(ainc[:, :], aexp[:, :], 1.0, None, ALU.add).then_inc(s_ainc, 1)
                dve.wait_ge(s_ainc, t + 1)
                nc.vector.reciprocal(rowbuf[:, b, 2 * D:2 * D + 1], ainc[:, :]).then_inc(s_alpha, 1)

            nc.vector.memset(ones[:], 1.0).then_inc(s_set, 1)
            nc.vector.memset(rowbuf[:, :, 2 * D:ROW], 0.0).then_inc(s_set, 1)
            dve.wait_ge(s_consts, CONSTS)
            for i in range(PER_TILE):
                nc.vector.tensor_copy(vblk[:, i, :, HEAD_DIM], c("head_in_stack", TT)).then_inc(s_set, 1)
            nc.vector.tensor_copy(ln1_bcast[:, :, :], ln1[:, 1, :].unsqueeze(2).to_broadcast([P, KX, TT])).then_inc(s_lnb, 1)
            nc.vector.tensor_tensor(shift[:, :], shift[:, :], shift2[:, :], ALU.add).then_inc(s_shift, 1)
            nc.vector.tensor_scalar(bqk_sb[:, 0:KD], bqk_sb[:, 0:KD], float(HEAD_DIM) ** -0.5, None, ALU.mult)\
                .then_inc(s_set, 1)
            dve.wait_ge(s_crow_ps, 1)
            nc.vector.tensor_tensor(tok_row[:, :], p_z, tok_row[:, :], ALU.add).then_inc(s_crow, 1)
            for k in range(KX):
                ins = nc.vector.tensor_scalar(tokw[:, k, :], tokw[:, k, :], ln1[:, 0, k:k + 1], None, ALU.mult)
            ins.then_inc(s_wfold, 1)
            dve.wait_ge(s_shift, 1)
            dve.wait_ge(s_crow, 1)

            x_moments(0, 0)
            x_norm(0, 0)
            z_moments(0)
            h_moments(0)
            h_norm(0)
            x_moments(0, 1)
            x_norm(1, 1)

            def step(j, b):
                t = 2 * j + b
                if not lacks(t, -1):
                    h1_moments(t - 1, 1 - b)
                if not lacks(t, 1):
                    z_moments(t + 1)
                if not lacks(t, -1):
                    xn_moments(t - 1)
                if not lacks(t, 1):
                    h_moments(t + 1)
                if not lacks(t, -1):
                    zn_row(j - 1 + b, 1 - b)
                softmax_in(t)
                if not lacks(t, 2):
                    x_moments(j + 1, b)
                v_out(t)
                if not lacks(t, 1):
                    h_norm(t + 1)
                if not lacks(t, -1):
                    keep_affinity(t - 1)
                if not lacks(t, 2):
                    x_norm(t + 2, b)
                if not lacks(t, -1):
                    alpha(t - 1, 1 - b)

            step(0, 0)
            step(0, 1)
            with dve.Fori(*PAIRS) as j:
                step(j, 0)
                step(j, 1)
            for t in range(TILES - 3, TILES):
                step(t // 2, t % 2)
            end = TILES - 1
            h1_moments(end, end % 2)
            xn_moments(end)
            zn_row(end // 2, end % 2)
            keep_affinity(end)
            alpha(end, end % 2)

            steps = [0]

            def then(ins):
                steps[0] += 1
                ins.then_inc(r_dve, 1)
                dve.wait_ge(r_dve, steps[0])

            def wide(ap, shape, *axes):
                for a in axes:
                    ap = ap.unsqueeze(a)
                return ap.to_broadcast(shape)

            ET = EXPERTS * TILES
            aff = aff_all[0:TT, :, :]
            te = [TT, TILES, EXPERTS]
            et = [TT, EXPERTS, TILES]
            then(nc.vector.tensor_reduce(r_max[0:TT, :], aff, AX.X, ALU.max))
            then(nc.vector.tensor_tensor(r_val[0:TT], aff, wide(r_max[0:TT, :], te, 2), ALU.is_ge))
            then(nc.vector.tensor_tensor(r_val[0:TT], r_val[0:TT], wide(c("rank", TT), te, 1), ALU.mult))
            then(nc.vector.tensor_reduce(r_first[0:TT, :], r_val[0:TT], AX.X, ALU.max))
            then(nc.vector.tensor_tensor(r_val[0:TT], r_val[0:TT], wide(r_first[0:TT, :], te, 2), ALU.is_equal))
            then(nc.vector.tensor_tensor(onehot[0:TT].rearrange("p e t -> p t e"), r_val[0:TT],
                                         wide(c("live", TT), te, 2), ALU.mult))
            nc.vector.tensor_copy(r_max[0:TT, :], r_max[0:TT, :]).then_inc(s_hot, 1)
            dve.wait_ge(s_count, 1)
            then(nc.vector.tensor_copy(tot[:, :, :].rearrange("p e t -> p (e t)"), p_count[:, ET:2 * ET]))
            then(nc.vector.tensor_tensor_scan(through[:, :, :].rearrange("p e t -> p (e t)"), c("restart"),
                                              tot[:, :, :].rearrange("p e t -> p (e t)"), 0.0, ALU.mult, ALU.add))
            shape = [P, EXPERTS, TOKENS // P + 1]
            then(nc.vector.tensor_tensor(r_cmp[:, :, :], through[:, :, TILES - 1].unsqueeze(2).to_broadcast(shape),
                                         wide(c("gt_slots"), shape, 1), ALU.is_gt))
            then(nc.vector.tensor_reduce(n_tiles[:, :], r_cmp[:, :, :], AX.X, ALU.add))
            then(nc.vector.tensor_tensor_scan(tile_end[:, :], ones[:, 0:EXPERTS], n_tiles[:, :], 0.0,
                                              ALU.mult, ALU.add))
            then(nc.vector.tensor_tensor(tile_start[:, :], tile_end[:, :], n_tiles[:, :], ALU.subtract))
            then(nc.vector.tensor_scalar(tile_start[:, :], tile_start[:, :], float(P), None, ALU.mult))
            then(nc.vector.tensor_tensor(place[0:TT], through[0:TT], tot[0:TT], ALU.subtract))
            then(nc.vector.tensor_tensor(place[0:TT], place[0:TT], wide(tile_start[0:TT, :], et, 2), ALU.add))
            then(nc.vector.tensor_tensor(place[0:TT], place[0:TT],
                                         p_count[0:TT, 0:ET].rearrange("p (e t) -> p e t", e=EXPERTS), ALU.add))
            then(nc.vector.tensor_tensor(place[0:TT], place[0:TT], onehot[0:TT], ALU.mult))
            then(nc.vector.tensor_reduce(pos[0:TT, :], place[0:TT].rearrange("p e t -> p t e"), AX.X, ALU.add))
            shape = [TT, TILES, SLOT_TILES - 1]
            then(nc.vector.tensor_tensor(r_ge[0:TT], wide(pos[0:TT, :], shape, 2), wide(c("ge_slots", TT), shape, 1),
                                         ALU.is_ge))
            then(nc.vector.tensor_reduce(slot_tile[0:TT, :], r_ge[0:TT], AX.X, ALU.add))
            then(nc.vector.scalar_tensor_tensor(slot_row[0:TT, :], slot_tile[0:TT, :], -float(P), pos[0:TT, :],
                                                ALU.mult, ALU.add))
            shape = [TT, TILES, SLOT_TILES]
            then(nc.vector.tensor_tensor(tile_hot[0:TT], wide(slot_tile[0:TT, :], shape, 2),
                                         wide(c("tile_no", TT), shape, 1), ALU.is_equal))
            then(nc.vector.tensor_tensor(tile_hot[0:TT], tile_hot[0:TT], wide(c("token", TT), shape, 2), ALU.mult))
            for t in range(TILES):
                ins = nc.vector.tensor_scalar(row_hot[0:TT, t, :], c("iota", TT), slot_row[0:TT, t:t + 1], None,
                                              ALU.is_equal)
            ins.then_inc(s_rowhot, 1)
            shape = [P, SLOT_TILES, EXPERTS]
            then(nc.vector.tensor_tensor(e_cmp[:, :, :], wide(c("tile_no"), shape, 2), wide(tile_end[:, :], shape, 1),
                                         ALU.is_ge))
            then(nc.vector.tensor_reduce(e_sum[:, :], e_cmp[:, :, :], AX.X, ALU.add))
            then(nc.vector.tensor_scalar(expert[:, :], e_sum[:, :], EXPERTS - 1.0, None, ALU.min))
            dve.wait_ge(s_slotp, 1)
            then(nc.vector.tensor_copy(slot[:, :], p_slot))
            then(nc.vector.tensor_scalar(gather_all[:, :], slot[:, :], 1.0, 0.0, ALU.subtract, ALU.max))
            then(nc.vector.tensor_scalar(empty[:, :], slot[:, :], 0.5, NO_TOKEN, ALU.is_lt, ALU.mult))
            then(nc.vector.tensor_scalar(slot_m1[:, :], slot[:, :], 1.0, None, ALU.subtract))
            then(nc.vector.tensor_tensor(scatter_all[:, :], slot_m1[:, :], empty[:, :], ALU.add))
            nc.vector.tensor_copy(slot_m1[:, :], slot_m1[:, :]).then_inc(s_route, 1)

            def columns(j, u):
                t = RING * j + u
                if above_zero(16 * j):
                    dve.wait_ge(s_gather[u], 16 * j)
                if above_zero(16 * j):
                    dve.wait_ge(s_scatter[u], 16 * j)
                nc.vector.tensor_copy(gather_idx[:, u:u + 1], gather_all[:, bass.ds(t, 1)])
                nc.vector.tensor_copy(scatter_idx[:, u:u + 1], scatter_all[:, bass.ds(t, 1)]).then_inc(s_idx, 1)
                e = dve.value_load(expert[0:1, bass.ds(t, 1)], min_val=0, max_val=EXPERTS - 1)
                if above_zero(KF * (t - RING + 1)):
                    dve.wait_ge(s_relu, KF * (t - RING + 1))
                nc.vector.tensor_copy(cur[:, u, :], cols_sb[:, bass.ds(e, 1), :].rearrange("p e n -> p (e n)"))\
                    .then_inc(s_cur, 1)
                return e

            def z_out(t, u):
                dve.wait_ge(s_zTp, t + 1)
                dve.wait_ge(s_cur, t + 1)
                if above_zero(t):
                    dve.wait_ge(s_up, t)
                for k in range(KD):
                    ins = nc.vector.tensor_scalar(zT[:, k, :], p_zT[:, k * P:(k + 1) * P], cur[:, u, k:k + 1],
                                                  cur[:, u, KD + k:KD + k + 1], ALU.mult, ALU.add)
                ins.then_inc(s_zTe, 1)

            def hidden_out(t):
                dve.wait_ge(s_up, t + 1)
                if above_zero(t):
                    dve.wait_ge(s_hidTp, t)
                nc.vector.tensor_copy(hid[:, :], p_up).then_inc(s_hid, 1)

            def finish(j, u):
                t = RING * j + u
                e = dve.value_load(expert[0:1, bass.ds(t, 1)], min_val=0, max_val=EXPERTS - 1)
                dve.wait_ge(s_down, t + 1)
                if above_zero(t):
                    dve.wait_ge(s_y, t)
                nc.vector.tensor_tensor(y1[:, :], p_down, b2_sb[:, bass.ds(e, 1), :].rearrange("p e n -> p (e n)"),
                                        ALU.add).then_inc(s_y1, 1)
                dve.wait_ge(s_y1, t + 1)
                dve.wait_ge(s_gather[u], 16 * (j + 1))
                if above_zero(16 * j):
                    dve.wait_ge(s_scatter[u], 16 * j)
                nc.vector.scalar_tensor_tensor(yout[:, u, :], y1[:, :], rows[:, u, 2 * D:2 * D + 1],
                                               rows[:, u, D:2 * D], ALU.mult, ALU.add).then_inc(s_y, 1)

            for u in range(RING):
                columns(0, u)
            z_out(0, 0)
            hidden_out(0)
            z_out(1, 1)

            def slot_step(j, u):
                t = RING * j + u
                whole = in_loop(t)
                if whole or t + 1 < SLOT_TILES:
                    hidden_out(t + 1)
                if whole or t + 2 < SLOT_TILES:
                    z_out(t + 2, (u + 2) % RING)
                finish(j, u)
                if whole or t + RING < SLOT_TILES:
                    columns(j + 1, u)

            for u in range(RING):
                slot_step(0, u)
            with dve.Fori(*SLOT_RINGS) as j:
                for u in range(RING):
                    slot_step(j, u)
            for t in range(SLOT_RINGS[1] * RING, SLOT_TILES):
                slot_step(t // RING, t % RING)


def _table():
    t = np.zeros((P, TABLE), np.float32)
    p = np.arange(P)[:, None]

    def put(name, value):
        a, w = COLS[name]
        t[:, a:a + w] = value

    put("ident", p == np.arange(P))
    put("before", p < np.arange(P))
    put("iota", np.arange(P))
    put("head_of_row", p // HEAD_DIM == np.arange(HC))
    put("head_in_stack", p // T == np.arange(HEADS) % PER_TILE)
    put("causal", np.where(np.arange(T) <= p % T, 0.0, MASKED))
    token = np.arange(TILES) * TT + p
    put("token", (token + 1) * (token < TOKENS))
    put("live", token < TOKENS)
    put("ge_slots", P * np.arange(1, SLOT_TILES))
    put("gt_slots", P * np.arange(TOKENS // P + 1))
    put("tile_no", np.arange(SLOT_TILES))
    put("rank", EXPERTS - np.arange(EXPERTS))
    put("restart", np.tile(np.arange(TILES) > 0, EXPERTS))
    return t


def _positions():
    ys, xs = np.meshgrid(np.arange(GRID), np.arange(GRID), indexing="ij")
    omega = np.arange(D // 4, dtype=np.float32) / np.float32(D // 4 - 1)
    omega = (np.float32(1.0) / np.float32(TEMPERATURE) ** omega).astype(np.float32)
    ys = ys.reshape(-1)[:, None].astype(np.float32) * omega
    xs = xs.reshape(-1)[:, None].astype(np.float32) * omega
    return np.concatenate([np.sin(xs), np.cos(xs), np.sin(ys), np.cos(ys)], axis=1).astype(np.float32)


def _chunks(a):
    return np.ascontiguousarray(a.reshape(-1, P, a.shape[-1]).transpose(1, 0, 2).reshape(P, -1))


def kernel(x, cls_tok, L0_tok_cls_token, L0_tok_cls_pos_embedding, L0_tok_ln1_g, L0_tok_ln1_b, L0_tok_W,
           L0_tok_bias, L0_tok_ln2_g, L0_tok_ln2_b, L0_attn_W, L0_attn_b, L0_ffn_centroids, L0_ffn_ln_g,
           L0_ffn_ln_b, L0_ffn_w1, L0_ffn_b1, L0_ffn_w2, L0_ffn_b2):
    import concourse.bacc as bacc
    from concourse.bass_utils import run_bass_kernel_spmd

    x = np.asarray(x).reshape(IMAGES, CHANNELS, GRID, PATCH, GRID, PATCH)
    patches = x.transpose(0, 2, 4, 3, 5, 1).reshape(IMAGES * PATCHES, PATCH_DIM)

    def row(a):
        return np.asarray(a).reshape(1, -1)

    def image_rows(first, second, patch):
        patch = np.broadcast_to(patch, (PATCHES, D))
        return np.tile(np.concatenate([first, second, patch]), (PER_TILE, 1))

    none = np.zeros((1, D), np.float32)
    attn_w = np.asarray(L0_attn_W)
    attn_b = np.asarray(L0_attn_b)
    cols = np.concatenate([np.asarray(a).reshape(EXPERTS, -1, P) for a in (L0_ffn_ln_g, L0_ffn_ln_b, L0_ffn_b1)],
                          axis=1)
    w1 = np.asarray(L0_ffn_w1).transpose(0, 2, 1).reshape(EXPERTS, KD, P, HIDDEN).transpose(0, 2, 1, 3)
    w2 = np.asarray(L0_ffn_w2).transpose(0, 2, 1).reshape(EXPERTS, KF, P, D).transpose(0, 2, 1, 3)
    inputs = {
        "x": patches,
        "tok_add": image_rows(row(cls_tok), row(L0_tok_cls_token), row(L0_tok_ln2_b)),
        "tok_add2": image_rows(none, row(L0_tok_cls_pos_embedding), _positions()),
        "tok_gain": image_rows(none, none, row(L0_tok_ln2_g)),
        "ln1_g": np.asarray(L0_tok_ln1_g).reshape(KX, P).T,
        "ln1_b": np.asarray(L0_tok_ln1_b).reshape(KX, P).T,
        "tok_w": _chunks(np.asarray(L0_tok_W)),
        "tok_bias": np.asarray(L0_tok_bias).reshape(D),
        "wqk": _chunks(attn_w[0:2 * D].T),
        "wv": _chunks(attn_w[2 * D:].T),
        "bqk": attn_b[0:2 * D].reshape(2 * KD, P).T,
        "bv": attn_b[2 * D:],
        "centroids": _chunks(np.asarray(L0_ffn_centroids).T),
        "expert_cols": cols.transpose(2, 0, 1).reshape(P, -1),
        "expert_b2": np.asarray(L0_ffn_b2).reshape(-1),
        "w1": w1.reshape(EXPERTS * P, -1),
        "w2": w2.reshape(EXPERTS * P, -1),
        "table": _table(),
    }
    nc = bacc.Bacc("TRN2", target_bir_lowering=False, num_devices=1)
    arrays, aps = {}, {}
    for name, a in inputs.items():
        a = np.ascontiguousarray(a)
        arrays[f"in_{name}"] = a
        aps[name] = nc.dram_tensor(f"in_{name}", a.shape, mybir.dt.from_np(a.dtype), kind="ExternalInput").ap()
    out = nc.dram_tensor("out", (TOKENS, D), F32, kind="ExternalOutput").ap()
    attention_tower(nc, out=out, **aps)
    r = run_bass_kernel_spmd(nc, [arrays], core_ids=[0])
    return r.results[0]["out"].reshape(IMAGES, T, D)
```

```python
from contextlib import ExitStack

import numpy as np

import concourse.bass as bass
from concourse import mybir

F32 = mybir.dt.float32
I32 = mybir.dt.int32
ALU = mybir.AluOpType
ACT = mybir.ActivationFunctionType
AX = mybir.AxisListType

IMAGES, CHANNELS, SIDE, PATCH = 32, 3, 96, 16
GRID = SIDE // PATCH
PATCHES = GRID * GRID
PATCH_DIM = CHANNELS * PATCH * PATCH
D = 256
HEADS, HEAD_DIM = 16, 16
EXPERTS, HIDDEN = 8, 1024
EPS = 1e-5
TEMPERATURE = 10000.0
P = 128

T = PATCHES + 2
PER_TILE = 3
TT = PER_TILE * T
TP = PER_TILE * PATCHES
TILES = -(-IMAGES // PER_TILE)
LAST_IMAGES = IMAGES - (TILES - 1) * PER_TILE
TOKENS = IMAGES * T
KX = PATCH_DIM // P
KD = D // P
KF = HIDDEN // P
HC = P // HEAD_DIM
GROUPS = -(-HEADS // PER_TILE)
VW = HEAD_DIM + 1
MASKED = -1e30

SLOT_TILES = (TOKENS - EXPERTS) // P + EXPERTS
ROW = 2 * D + 8
NO_TOKEN = 4096.0
RING = 3

_WIDTHS = [("ident", P), ("before", P), ("iota", P), ("head_of_row", HC), ("head_in_stack", HEADS),
           ("causal", T), ("token", TILES), ("live", TILES), ("ge_slots", SLOT_TILES - 1),
           ("gt_slots", TOKENS // P + 1), ("tile_no", SLOT_TILES), ("rank", EXPERTS),
           ("restart", EXPERTS * TILES)]
COLS = {}
_at = 0
for _name, _width in _WIDTHS:
    COLS[_name] = (_at, _width)
    _at += _width
TABLE = _at


def attention_tower(nc, x, tok_add, tok_add2, tok_gain, ln1_gb, tok_w, tok_bias, wqk, wv, bqk, bv,
                    centroids, expert_cols, expert_b2, w1, w2, table, out):
    rows_dram = nc.dram_tensor("token_rows", (TOKENS, ROW), F32)
    with ExitStack() as ctx:
        def sb(name, shape, dt=F32):
            return ctx.enter_context(nc.sbuf_tensor(name, shape, dt))

        def sem(name):
            return ctx.enter_context(nc.semaphore(name))

        tab = sb("tab", [P, TABLE])
        ones = sb("ones", [P, P])
        w1_sb = sb("w1_sb", [P, EXPERTS, KD, HIDDEN])
        w2_sb = sb("w2_sb", [P, EXPERTS, KF, D])
        b2_sb = sb("b2_sb", [P, EXPERTS, D])
        cols_sb = sb("cols_sb", [P, EXPERTS, 2 * KD + KF])
        cent_sb = sb("cent_sb", [P, KD, EXPERTS])
        aff_all = sb("aff_all", [P, TILES, EXPERTS])

        phase_a = ExitStack()

        def sa(name, shape, dt=F32):
            return phase_a.enter_context(nc.sbuf_tensor(name, shape, dt))

        tokw = sa("tokw", [P, KX, D])
        tok_row = sa("tok_row", [TT, D])
        gain = sa("gain", [TT, D])
        shift = sa("shift", [TT, D])
        ln1 = sa("ln1", [P, 2, KX])
        wqk_sb = sa("wqk_sb", [P, KD, 2 * D])
        wv_sb = sa("wv_sb", [P, KD, D])
        bqk_sb = sa("bqk_sb", [P, 4])
        bv_sb = sa("bv_sb", [TT, D])
        xin = sa("xin", [TP, 2, PATCH_DIM])
        xT = sa("xT", [P, KX, TT])
        z = sa("z", [TT, D])
        h = sa("h", [TT, D])
        hb = sa("hb", [TT, 2, D])
        hn = sa("hn", [TT, D])
        hT = sa("hT", [P, KD, PER_TILE, PER_TILE, T])
        qT = sa("qT", [P, KD, PER_TILE * (TT + T)])
        kT = sa("kT", [P, KD, TT])
        kblk = sa("kblk", [P, KD, PER_TILE, HC, T])
        vblk = sa("vblk", [TT, PER_TILE, HEADS, VW])
        prob = sa("prob", [TT, HEADS, T])
        probT = sa("probT", [TT, GROUPS, PER_TILE * (TT + T)])
        h1 = sa("h1", [TT, D])
        shift2 = h1
        xn = sa("xn", [TT, D])
        xnT = sa("xnT", [P, KD, TT])
        stats = sa("stats", [TT, 5, 2, 6])
        mv = sa("mv", [TT, 5, 2])
        eps_col = sa("eps_col", [TT, 1])
        half_col = sa("half_col", [TT, 1])
        var_eps = sa("var_eps", [TT, 5])
        rstd = sa("rstd", [TT, 5])
        smax = sa("smax", [TT, HEADS])
        srec = sa("srec", [TT, HEADS])
        amax = sa("amax", [TT, 1])
        aexp = sa("aexp", [TT, 1])
        ainc = sa("ainc", [TT, 1])
        rowbuf = sa("rowbuf", [TT, 2, ROW])
        phase_a.close()

        onehot = sb("onehot", [P, EXPERTS, TILES])
        r_max = sb("r_max", [P, TILES])
        r_val = sb("r_val", [P, TILES, EXPERTS])
        r_first = sb("r_first", [P, TILES])
        through = sb("through", [P, EXPERTS, TILES])
        tot = sb("tot", [P, EXPERTS, TILES])
        r_cmp = sb("r_cmp", [P, EXPERTS, TOKENS // P + 1])
        n_tiles = sb("n_tiles", [P, EXPERTS])
        tile_end = sb("tile_end", [P, EXPERTS])
        tile_start = sb("tile_start", [P, EXPERTS])
        place = sb("place", [P, EXPERTS, TILES])
        pos = sb("pos", [P, TILES])
        r_ge = sb("r_ge", [P, TILES, SLOT_TILES - 1])
        slot_tile = sb("slot_tile", [P, TILES])
        slot_row = sb("slot_row", [P, TILES])
        tile_hot = sb("tile_hot", [P, TILES, SLOT_TILES])
        row_hot = sb("row_hot", [P, TILES, P])
        slot = sb("slot", [P, SLOT_TILES])
        slot_m1 = sb("slot_m1", [P, SLOT_TILES])
        empty = sb("empty", [P, SLOT_TILES])
        gather_all = sb("gather_all", [P, SLOT_TILES], I32)
        scatter_all = sb("scatter_all", [P, SLOT_TILES], I32)
        e_cmp = sb("e_cmp", [P, SLOT_TILES, EXPERTS])
        e_sum = sb("e_sum", [P, SLOT_TILES])
        expert = sb("expert", [P, SLOT_TILES], I32)

        cur = sb("cur", [P, RING, 2 * KD + KF])
        rows = sb("rows", [P, RING, ROW])
        zT = sb("zT", [P, KD, P])
        w1_cur = sb("w1_cur", [P, RING, KD, HIDDEN])
        b2_cur = sb("b2_cur", [P, RING, D])
        hidT = sb("hidT", [P, RING, KF, P])
        y1 = sb("y1", [P, D])
        yout = sb("yout", [P, RING, D])

        ps = ctx.enter_context(nc.psum_tensor("ps", [P, 8, 512], F32))

        def c(name, n=P):
            a, w = COLS[name]
            return tab[0:n, a:a + w]

        ident = c("ident")

        def bank(n, width, parts=P, banks=1):
            return ps[0:parts, n:n + banks, :].rearrange("p b n -> p (b n)")[:, 0:width]

        p_xT = ps[:, 0:2, 0:3 * TP]
        p_v = bank(0, PER_TILE * D, TT, 2)
        p_z = bank(2, D, TT)
        p_hT = bank(3, KD * TT)
        p_xnT = ps[:, 2, D:D + KD * TT]
        p_qk = bank(4, 4 * TT)
        p_o = bank(5, HEADS * VW, TT)
        p_aff = ps[0:TT, 5, HEADS * VW:HEADS * VW + EXPERTS]
        p_s = ps[0:TT, 6:8, 0:HC * T]
        p_pT = [ps[0:TT, 6, 0:4 * TT], ps[0:TT, 7, 0:2 * TT]]
        p_count = bank(2, 2 * EXPERTS * TILES)
        p_slot = bank(4, SLOT_TILES)
        p_zT = bank(0, KD * P)
        p_hidT = bank(1, KF * P, P, 2)
        p_down = bank(7, D)

        s_table = sem("table_loaded")
        s_embed_w = sem("embedding_weights_loaded")
        s_rows = sem("token_rows_loaded")
        s_attn_w = sem("attention_weights_loaded")
        s_expert_c = sem("expert_consts_loaded")
        s_w = sem("experts_loaded")
        s_set = sem("buffers_set")
        s_bq = sem("query_bias_scaled")
        s_shift = sem("shift_ready")
        s_x = [sem("x_loaded_even"), sem("x_loaded_odd")]
        s_xstat = sem("x_stats")
        s_xmv = sem("x_moments")
        s_xn = sem("x_normalised")
        s_xTp = sem("x_transposed")
        s_xT = sem("xT_ready")
        s_zp = sem("z_summed")
        s_z = sem("z_ready")
        s_zstat = sem("z_stats")
        s_zmv = sem("z_moments")
        s_zn = sem("z_normalised")
        s_zg = sem("z_scaled")
        s_h = sem("h_ready")
        s_hstat = sem("h_stats")
        s_hmv = sem("h_moments")
        s_hn = sem("h_normalised")
        s_hb = sem("h_plus_bv")
        s_hTp = sem("h_transposed")
        s_hT = sem("hT_ready")
        s_qkp = sem("qk_projected")
        s_q = sem("q_ready")
        s_k = sem("k_ready")
        s_kblk = sem("k_blocks_ready")
        s_vp = sem("v_projected")
        s_v = sem("v_blocks_ready")
        s_sp = sem("scores_summed")
        s_sm = sem("scores_masked")
        s_smax = sem("score_max")
        s_sub = sem("scores_shifted")
        s_exp = sem("exp_done")
        s_pTp = sem("probs_transposed")
        s_pT = sem("probT_ready")
        s_o = sem("attention_summed")
        s_rec = sem("sums_inverted")
        s_on = sem("attention_scaled")
        s_h1 = sem("h1_ready")
        s_h1stat = sem("h1_stats")
        s_h1mv = sem("h1_moments")
        s_x2 = sem("xn_ready")
        s_base = sem("base_ready")
        s_x2stat = sem("xn_stats")
        s_x2mv = sem("xn_moments")
        s_row = sem("row_zn_ready")
        s_xnTp = sem("xn_transposed")
        s_xnT = sem("xnT_ready")
        s_affp = sem("affinity_summed")
        s_aff = sem("affinity_kept")
        s_amax = sem("affinity_max")
        s_aexp = sem("alpha_exp")
        s_ainc = sem("alpha_plus_one")
        s_alpha = sem("alpha_ready")
        s_stored = [sem("rows_stored_even"), sem("rows_stored_odd")]
        s_var = [sem(f"variance_eps_{n}") for n in range(5)]
        s_rstd = [sem(f"rstd_{n}") for n in range(5)]

        s_passed_dve = sem("waits_passed_vector")
        SETS = 5 + 2 + PER_TILE
        LN_X, LN_Z, LN_H, LN_H1, LN_XN = range(5)

        def in_loop(t):
            return not isinstance(t, int)

        def above_zero(count):
            return in_loop(count) or count > 0

        def at(q, b, k):
            return q + (b + k) // 2, (b + k) % 2

        def exists(q, b, k=0):
            return in_loop(q) or 0 <= 2 * q + b + k < TILES

        def last(t):
            return not in_loop(t) and t == TILES - 1

        PAIRS = (1, (TILES - 3) // 2)
        SLOT_RINGS = (1, (SLOT_TILES - RING) // RING)

        r_dve = sem("routing_step")
        s_hot = sem("onehot_ready")
        s_count = sem("counts_summed")
        s_rowhot = sem("slot_hots_ready")
        s_slotp = sem("slots_summed")
        s_route = sem("routing_ready")
        s_gather = [sem(f"rows_gathered_{n}") for n in range(RING)]
        s_scatter = [sem(f"rows_scattered_{n}") for n in range(RING)]
        s_cur = sem("expert_columns_ready")
        s_zTp = sem("zn_transposed")
        s_zTe = sem("zT_ready")
        s_w1cur = sem("expert_w1_ready")
        s_b2cur = sem("expert_b2_ready")
        s_up = sem("up_summed")
        s_relu = sem("hidden_relu")
        s_down = sem("down_summed")
        s_y1 = sem("y_plus_b2")
        s_y = sem("y_ready")

        block = ctx.enter_context(nc.Block())

        @block.sync
        def _(sp):
            def load_x(q, b):
                t = 2 * q + b
                if above_zero(t - 1):
                    sp.wait_ge(s_xTp, t - 1)
                n = LAST_IMAGES * PATCHES if last(t) else TP
                sp.dma_start(xin[0:n, b, :], x[bass.ds(t * TP, n), :]).then_inc(s_x[b], 16)

            def load_expert(e):
                sp.dma_start(w1_sb[:, bass.ds(e, 1), :, :].rearrange("p e c n -> p (e c n)"),
                             w1[bass.ds(e * P, P), :]).then_inc(s_w, 16)
                sp.dma_start(w2_sb[:, bass.ds(e, 1), :, :].rearrange("p e c n -> p (e c n)"),
                             w2[bass.ds(e * P, P), :]).then_inc(s_w, 16)

            def store_rows(q, b):
                t = 2 * q + b
                sp.wait_ge(s_row, t + 1)
                sp.wait_ge(s_base, t + 1)
                sp.wait_ge(s_alpha, t + 1)
                n = LAST_IMAGES * T if last(t) else TT
                sp.dma_start(rows_dram[bass.ds(t * TT, n), :], rowbuf[0:n, b, :]).then_inc(s_stored[b], 16)

            def step(q, b):
                t = 2 * q + b
                if exists(q, b, 3):
                    load_x(*at(q, b, 3))
                if in_loop(t) or t < EXPERTS:
                    load_expert(t)
                if exists(q, b, -2):
                    store_rows(*at(q, b, -2))

            load_x(0, 0)
            sp.dma_start(tok_row[:, :], tok_bias.partition_broadcast(TT)).then_inc(s_rows, 16)
            sp.dma_start(gain[:, :], tok_gain).then_inc(s_rows, 16)
            sp.dma_start(shift[:, :], tok_add).then_inc(s_rows, 16)
            sp.dma_start(shift2[:, :], tok_add2).then_inc(s_rows, 16)
            load_x(0, 1)
            sp.dma_start(wqk_sb[:, :, :].rearrange("p c n -> p (c n)"), wqk).then_inc(s_attn_w, 16)
            sp.dma_start(bqk_sb[:, :], bqk).then_inc(s_attn_w, 16)
            sp.dma_start(wv_sb[:, :, :].rearrange("p c n -> p (c n)"), wv).then_inc(s_attn_w, 16)
            sp.dma_start(bv_sb[:, :], bv.partition_broadcast(TT)).then_inc(s_attn_w, 16)
            load_x(1, 0)
            sp.dma_start(cent_sb[:, :, :].rearrange("p c n -> p (c n)"), centroids).then_inc(s_expert_c, 16)
            sp.dma_start(cols_sb[:, :, :].rearrange("p e n -> p (e n)"), expert_cols).then_inc(s_expert_c, 16)
            sp.dma_start(b2_sb[:, :, :].rearrange("p e n -> p (e n)"), expert_b2.partition_broadcast(P))\
                .then_inc(s_expert_c, 16)
            step(0, 0)
            step(0, 1)
            step(1, 0)
            with sp.Fori(PAIRS[0], PAIRS[1] - 1) as j:
                step(j, 1)
                step(j + 1, 0)
            for t in range(2 * PAIRS[1] - 1, TILES):
                step(t // 2, t % 2)
            for t in (TILES - 2, TILES - 1):
                store_rows(t // 2, t % 2)

        @block.gpsimd
        def _(pool):
            def inv_std(n, moments, t, parts=TT):
                pool.wait_ge(moments, t + 1)
                nc.gpsimd.tensor_tensor(var_eps[0:parts, n:n + 1], mv[0:parts, n, 1:2], eps_col[0:parts, :],
                                        ALU.add).then_inc(s_var[n], 1)
                pool.wait_ge(s_var[n], t + 1)
                nc.gpsimd.tensor_tensor(rstd[0:parts, n:n + 1], var_eps[0:parts, n:n + 1], half_col[0:parts, :],
                                        ALU.pow).then_inc(s_rstd[n], 1)

            def key_blocks(q, b, ch):
                t = 2 * q + b
                pool.wait_ge(s_k, t + 1)
                if above_zero(t):
                    pool.wait_ge(s_sp, t)
                for i in range(PER_TILE):
                    ins = nc.gpsimd.tensor_tensor(
                        kblk[:, ch, i, :, :],
                        kT[:, ch, i * T:(i + 1) * T].unsqueeze(1).to_broadcast([P, HC, T]),
                        c("head_of_row").unsqueeze(2).to_broadcast([P, HC, T]), ALU.mult)
                ins.then_inc(s_kblk, 1)

            def base(q, b):
                pool.wait_ge(s_x2, 2 * q + b + 1)
                if above_zero(q):
                    pool.wait_ge(s_stored[b], 16 * q)
                nc.gpsimd.tensor_tensor(rowbuf[:, b, D:2 * D], h1[:, :], xn[:, :], ALU.add).then_inc(s_base, 1)

            def value_bias(q, b):
                t = 2 * q + b
                pool.wait_ge(s_h, t + 1)
                if above_zero(t - 1):
                    pool.wait_ge(s_h1, t - 1)
                nc.gpsimd.tensor_tensor(hb[:, b, :], h[:, :], bv_sb[:, :], ALU.add).then_inc(s_hb, 1)

            nc.gpsimd.memset(eps_col[:], EPS).then_inc(s_set, 1)
            nc.gpsimd.memset(half_col[:], -0.5).then_inc(s_set, 1)
            nc.gpsimd.memset(xT[:], 0.0).then_inc(s_set, 1)
            nc.gpsimd.memset(qT[:], 0.0).then_inc(s_set, 1)
            nc.gpsimd.memset(probT[:], 0.0).then_inc(s_set, 1)
            pool.wait_ge(s_set, SETS)

            inv_std(LN_X, s_xmv, 0, TP)
            inv_std(LN_X, s_xmv, 1, TP)
            inv_std(LN_Z, s_zmv, 0)
            inv_std(LN_H, s_hmv, 0)
            pool.wait_ge(s_table, 16)
            pool.wait_ge(s_attn_w, 16 * 4)
            value_bias(0, 0)

            def step(q, b):
                t = 2 * q + b
                if exists(q, b, 2):
                    inv_std(LN_X, s_xmv, t + 2, TP)
                key_blocks(q, b, 0)
                if exists(q, b, 1):
                    inv_std(LN_Z, s_zmv, t + 1)
                key_blocks(q, b, 1)
                if exists(q, b, 1):
                    inv_std(LN_H, s_hmv, t + 1)
                if exists(q, b, -1):
                    inv_std(LN_H1, s_h1mv, t - 1)
                if exists(q, b, 1):
                    value_bias(*at(q, b, 1))
                if exists(q, b, -1):
                    inv_std(LN_XN, s_x2mv, t - 1)
                    base(*at(q, b, -1))

            step(0, 0)
            step(0, 1)
            step(1, 0)
            with pool.Fori(*PAIRS) as j:
                step(j, 1)
                step(j + 1, 0)
            for t in range(2 * PAIRS[1] + 1, TILES):
                step(t // 2, t % 2)
            inv_std(LN_H1, s_h1mv, TILES - 1)
            inv_std(LN_XN, s_x2mv, TILES - 1)
            base((TILES - 1) // 2, (TILES - 1) % 2)

            pool.wait_ge(s_stored[0], 16 * -(-TILES // 2))
            pool.wait_ge(s_stored[1], 16 * (TILES // 2))

            def gather(t):
                if above_zero(t - RING + 1):
                    pool.wait_ge(s_y, t - RING + 1)
                nc.gpsimd.indirect_dma_start(
                    rows[:, t % RING, :], None, rows_dram[:, :],
                    bass.IndirectOffsetOnAxis(ap=gather_all[:, t:t + 1], axis=0)).then_inc(s_gather[t % RING], 16)

            pool.wait_ge(s_route, 1)
            for t in range(RING):
                gather(t)
            for t in range(SLOT_TILES):
                if t + RING < SLOT_TILES:
                    gather(t + RING)
                pool.wait_ge(s_y, t + 1)
                nc.gpsimd.indirect_dma_start(
                    out, bass.IndirectOffsetOnAxis(ap=scatter_all[:, t:t + 1], axis=0), yout[:, t % RING, :], None,
                    bounds_check=TOKENS - 1, oob_is_err=False).then_inc(s_scatter[t % RING], 16)
            for u in range(RING):
                pool.wait_ge(s_scatter[u], 16 * len(range(u, SLOT_TILES, RING)))

        @block.scalar
        def _(act):
            act.dma_start(tab[:, :], table).then_inc(s_table, 16)
            act.dma_start(tokw[:, :, :].rearrange("p c n -> p (c n)"), tok_w).then_inc(s_embed_w, 16)
            act.dma_start(ln1[:, :, :].rearrange("p a c -> p (a c)"), ln1_gb).then_inc(s_embed_w, 16)

            def x_out(t):
                act.wait_ge(s_xTp, t + 1)
                if above_zero(t):
                    act.wait_ge(s_zp, t)
                for k in range(KX):
                    ins = nc.scalar.activation(
                        xT[:, k, :].rearrange("p (i k) -> p i k", i=PER_TILE)[:, :, 2:T],
                        p_xT[:, k // 3, (k % 3) * TP:(k % 3 + 1) * TP].rearrange("p (i k) -> p i k", i=PER_TILE),
                        ACT.Identity, bias=ln1[:, 1, k:k + 1], scale=ln1[:, 0, k:k + 1])
                ins.then_inc(s_xT, 1)

            def h_out(t):
                act.wait_ge(s_hTp, t + 1)
                if above_zero(t):
                    act.wait_ge(s_vp, t)
                for k in range(KD):
                    source = p_hT[:, k * TT:(k + 1) * TT].rearrange("p (i k) -> p i k", i=PER_TILE)
                    ins = nc.scalar.activation(
                        hT[:, k], source.unsqueeze(2).to_broadcast([P, PER_TILE, PER_TILE, T]), ACT.Copy)
                ins.then_inc(s_hT, 1)

            def k_out(t):
                act.wait_ge(s_qkp, t + 1)
                if above_zero(t):
                    act.wait_ge(s_kblk, KD * t)
                for ch in range(KD):
                    ins = nc.scalar.activation(kT[:, ch, :], p_qk[:, (KD + ch) * TT:(KD + ch + 1) * TT],
                                               ACT.Identity, bias=bqk_sb[:, KD + ch:KD + ch + 1])
                ins.then_inc(s_k, 1)

            def q_out(t):
                if above_zero(t):
                    act.wait_ge(s_sp, t)
                blocks = qT[:, :, :].rearrange("p c (i s) -> p c i s", i=PER_TILE)[:, :, :, 0:T]
                for ch in range(KD):
                    ins = nc.scalar.activation(
                        blocks[:, ch], p_qk[:, ch * TT:(ch + 1) * TT].rearrange("p (i k) -> p i k", i=PER_TILE),
                        ACT.Identity, bias=bqk_sb[:, ch:ch + 1], scale=float(HEAD_DIM) ** -0.5)
                ins.then_inc(s_q, 1)

            def exps(t):
                act.wait_ge(s_sub, t + 1)
                nc.scalar.activation(prob[:, :, :], prob[:, :, :], ACT.Exp).then_inc(s_exp, 1)

            def prob_out(t):
                act.wait_ge(s_pTp, t + 1)
                if above_zero(t):
                    act.wait_ge(s_o, t)
                blocks = probT[:, :, :].rearrange("p g (i s) -> p g i s", i=PER_TILE)[:, :, :, 0:T]
                nc.scalar.activation(blocks[:, 0:4], p_pT[0].rearrange("p (g i k) -> p g i k", g=4, i=PER_TILE), ACT.Copy)
                nc.scalar.activation(blocks[:, 4], p_pT[1][:, 0:TT].rearrange("p (i k) -> p i k", i=PER_TILE), ACT.Copy)
                nc.scalar.activation(blocks[0:T, 5], p_pT[1][0:T, TT:2 * TT].rearrange("p (i k) -> p i k", i=PER_TILE),
                                     ACT.Copy).then_inc(s_pT, 1)

            def xn_out(t):
                act.wait_ge(s_xnTp, t + 1)
                if above_zero(t):
                    act.wait_ge(s_affp, t)
                nc.scalar.activation(xnT[:, :, :].rearrange("p c n -> p (c n)"), p_xnT, ACT.Copy).then_inc(s_xnT, 1)

            def alpha_exp(t):
                act.wait_ge(s_amax, t + 1)
                nc.scalar.activation(aexp[:, :], amax[:, :], ACT.Exp, scale=-1.0).then_inc(s_aexp, 1)

            act.wait_ge(s_set, SETS)
            nc.scalar.activation(smax[:, 0:1], half_col[:, :], ACT.Exp)
            act.wait_ge(s_embed_w, 16 * 2)
            x_out(0)
            h_out(0)
            x_out(1)
            act.wait_ge(s_attn_w, 16 * 4)
            act.wait_ge(s_bq, 1)

            def step(q, b):
                t = 2 * q + b
                if exists(q, b, -1):
                    prob_out(t - 1)
                k_out(t)
                q_out(t)
                if exists(q, b, -2):
                    alpha_exp(t - 2)
                exps(t)
                if exists(q, b, 1):
                    h_out(t + 1)
                if exists(q, b, -1):
                    xn_out(t - 1)
                if exists(q, b, 2):
                    x_out(t + 2)

            step(0, 0)
            step(0, 1)
            step(1, 0)
            with act.Fori(*PAIRS) as j:
                step(j, 1)
                step(j + 1, 0)
            for t in range(2 * PAIRS[1] + 1, TILES):
                step(t // 2, t % 2)
            prob_out(TILES - 1)
            alpha_exp(TILES - 2)
            xn_out(TILES - 1)
            alpha_exp(TILES - 1)

            def slot_step(j, u):
                t = RING * j + u
                act.wait_ge(s_up, KF * t + KF // 2)
                act.wait_ge(s_cur, t + 1)
                if above_zero(t - RING + 1):
                    act.wait_ge(s_down, t - RING + 1)
                for k in range(KF):
                    if k == KF // 2:
                        act.wait_ge(s_up, KF * (t + 1))
                    nc.scalar.activation(hidT[:, u, k, :], p_hidT[:, k * P:(k + 1) * P], ACT.Relu,
                                         bias=cur[:, u, 2 * KD + k:2 * KD + k + 1]).then_inc(s_relu, 1)

            for u in range(RING):
                slot_step(0, u)
            with act.Fori(*SLOT_RINGS) as j:
                for u in range(RING):
                    slot_step(j, u)
            for t in range(SLOT_RINGS[1] * RING, SLOT_TILES):
                slot_step(t // RING, t % RING)

        @block.tensor
        def _(pe):
            def x_turn(t, b):
                pe.wait_ge(s_xn, t + 1)
                if above_zero(t - 1):
                    pe.wait_ge(s_v, t - 1)
                for k in range(KX):
                    ins = nc.tensor.transpose(p_xT[:, k // 3, (k % 3) * TP:(k % 3 + 1) * TP],
                                              xin[:, b, k * P:(k + 1) * P], ident[0:TP, 0:TP])
                ins.then_inc(s_xTp, 1)

            def embed(t):
                pe.wait_ge(s_xT, t + 1)
                if above_zero(t):
                    pe.wait_ge(s_z, t)
                if above_zero(t - 2):
                    pe.wait_ge(s_xnT, t - 2)
                for k in range(KX):
                    ins = nc.tensor.matmul(p_z, xT[:, k, :], tokw[:, k, :], start=k == 0, stop=k == KX - 1)
                ins.then_inc(s_zp, 1)

            def h_turn(t):
                pe.wait_ge(s_hn, t + 1)
                if above_zero(t):
                    pe.wait_ge(s_hT, t)
                for k in range(KD):
                    ins = nc.tensor.transpose(p_hT[:, k * TT:(k + 1) * TT], hn[:, k * P:(k + 1) * P], ident[0:TT, 0:TT])
                ins.then_inc(s_hTp, 1)

            def project_qk(t):
                pe.wait_ge(s_hT, t + 1)
                if above_zero(t):
                    pe.wait_ge(s_q, t)
                if above_zero(t):
                    pe.wait_ge(s_k, t)
                for m in range(2 * KD):
                    for k in range(KD):
                        ins = nc.tensor.matmul(p_qk[:, m * TT:(m + 1) * TT], wqk_sb[:, k, m * P:(m + 1) * P],
                                               hT[:, k, :, 0, :], start=k == 0, stop=k == KD - 1)
                ins.then_inc(s_qkp, 1)

            def project_v(t):
                pe.wait_ge(s_xT, t + 2 if in_loop(t) else min(t + 2, TILES))
                for i in range(PER_TILE):
                    for k in range(KD):
                        ins = nc.tensor.matmul(
                            p_v[:, i * D:(i + 1) * D],
                            hT[:, k, i, :, :].rearrange("p r k -> p (r k)"),
                            wv_sb[:, k, :], start=k == 0, stop=k == KD - 1)
                ins.then_inc(s_vp, 1)

            def scores(t):
                pe.wait_ge(s_q, t + 1)
                if above_zero(t):
                    pe.wait_ge(s_pT, t)
                for ch in range(KD):
                    pe.wait_ge(s_kblk, KD * t + ch + 1)
                    for i in range(PER_TILE):
                        ins = nc.tensor.matmul(p_s[:, ch, :], qT[:, ch, i * TT:(i + 1) * TT],
                                               kblk[:, ch, i, :, :].rearrange("p a k -> p (a k)"),
                                               start=i == 0, stop=i == PER_TILE - 1)
                ins.then_inc(s_sp, 1)

            def prob_turn(t):
                pe.wait_ge(s_exp, t + 1)
                flat = prob[:, :, :].rearrange("p a k -> p (a k)")
                for g in range(GROUPS):
                    n = min(TT, HEADS * T - g * TT)
                    ins = nc.tensor.transpose(p_pT[g // 4][0:n, (g % 4) * TT:(g % 4 + 1) * TT],
                                              flat[:, g * TT:g * TT + n], ident[0:TT, 0:TT])
                ins.then_inc(s_pTp, 1)

            def attend(t):
                pe.wait_ge(s_pT, t + 1)
                pe.wait_ge(s_v, t + 1)
                if above_zero(t):
                    pe.wait_ge(s_on, t)
                    pe.wait_ge(s_aff, t)
                for g in range(GROUPS):
                    heads = min(PER_TILE, HEADS - g * PER_TILE)
                    rows_g = heads * T
                    for i in range(PER_TILE):
                        ins = nc.tensor.matmul(
                            p_o[:, g * PER_TILE * VW:(g * PER_TILE + heads) * VW],
                            probT[0:rows_g, g, i * TT:(i + 1) * TT],
                            vblk[0:rows_g, i, g * PER_TILE:g * PER_TILE + heads, :].rearrange("p a v -> p (a v)"),
                            start=i == 0, stop=i == PER_TILE - 1)
                ins.then_inc(s_o, 1)

            def xn_turn(t):
                pe.wait_ge(s_x2, t + 1)
                pe.wait_ge(s_z, t + 3 if in_loop(t) else min(t + 3, TILES))
                for k in range(KD):
                    ins = nc.tensor.transpose(p_xnT[:, k * TT:(k + 1) * TT], xn[:, k * P:(k + 1) * P], ident[0:TT, 0:TT])
                ins.then_inc(s_xnTp, 1)

            def affinity(t):
                pe.wait_ge(s_xnT, t + 1)
                pe.wait_ge(s_on, t + 1)
                for k in range(KD):
                    ins = nc.tensor.matmul(p_aff, xnT[:, k, :], cent_sb[:, k, :], start=k == 0, stop=k == KD - 1)
                ins.then_inc(s_affp, 1)

            pe.wait_ge(s_set, SETS)
            pe.wait_ge(s_table, 16)
            x_turn(0, 0)
            pe.wait_ge(s_embed_w, 16 * 2)
            embed(0)
            x_turn(1, 1)
            h_turn(0)
            pe.wait_ge(s_attn_w, 16 * 4)
            pe.wait_ge(s_expert_c, 16 * 3)

            def step(q, b):
                t = 2 * q + b
                project_qk(t)
                if exists(q, b, -2):
                    affinity(t - 2)
                if exists(q, b, 1):
                    embed(t + 1)
                if exists(q, b, -1):
                    attend(t - 1)
                scores(t)
                project_v(t)
                prob_turn(t)
                if exists(q, b, 1):
                    h_turn(t + 1)
                if exists(q, b, -1):
                    xn_turn(t - 1)
                if exists(q, b, 2):
                    x_turn(t + 2, b)

            step(0, 0)
            step(0, 1)
            step(1, 0)
            with pe.Fori(*PAIRS) as j:
                step(j, 1)
                step(j + 1, 0)
            for t in range(2 * PAIRS[1] + 1, TILES):
                step(t // 2, t % 2)
            affinity(TILES - 2)
            attend(TILES - 1)
            xn_turn(TILES - 1)
            affinity(TILES - 1)

            ET = EXPERTS * TILES
            hot = onehot[0:TT, :, :].rearrange("p e t -> p (e t)")
            pe.wait_ge(s_hot, 1)
            nc.tensor.matmul(p_count[0:TT, 0:ET], c("before", TT)[:, 0:TT], hot, start=True, stop=True)
            nc.tensor.matmul(p_count[:, ET:2 * ET], ones[0:TT, :], hot, start=True, stop=True).then_inc(s_count, 1)
            pe.wait_ge(s_rowhot, 1)
            for t in range(TILES):
                ins = nc.tensor.matmul(p_slot, row_hot[0:TT, t, :], tile_hot[0:TT, t, :],
                                       start=t == 0, stop=t == TILES - 1)
            ins.then_inc(s_slotp, 1)

            def zn_turn(j, u):
                t = RING * j + u
                pe.wait_ge(s_gather[u], 16 * (j + 1))
                if above_zero(t):
                    pe.wait_ge(s_zTe, t)
                for k in range(KD):
                    ins = nc.tensor.transpose(p_zT[:, k * P:(k + 1) * P], rows[:, u, k * P:(k + 1) * P], ident)
                ins.then_inc(s_zTp, 1)

            def up(t, u):
                pe.wait_ge(s_zTe, t + 1)
                pe.wait_ge(s_w1cur, t + 1)
                for m in range(KF):
                    if m % (KF // 2) == 0 and above_zero(KF * t):
                        pe.wait_ge(s_relu, KF * (t - 1) + m + KF // 2)
                    for k in range(KD):
                        ins = nc.tensor.matmul(p_hidT[:, m * P:(m + 1) * P], w1_cur[:, u, k, m * P:(m + 1) * P],
                                               zT[:, k, :], start=k == 0, stop=k == KD - 1)
                    ins.then_inc(s_up, 1)

            def down(t, u, e, ks):
                for k in ks:
                    if k == 0 and above_zero(t):
                        pe.wait_ge(s_y1, t)
                    pe.wait_ge(s_relu, KF * t + k + 1)
                    ins = nc.tensor.matmul(p_down, hidT[:, u, k, :],
                                           w2_sb[:, bass.ds(e, 1), k, :].rearrange("p e n -> p (e n)"),
                                           start=k == 0, stop=k == KF - 1)
                if k == KF - 1:
                    ins.then_inc(s_down, 1)

            pe.wait_ge(s_w, 16 * 2 * EXPERTS)
            pe.wait_ge(s_route, 1)
            zn_turn(0, 0)
            up(0, 0)
            zn_turn(0, 1)

            def slot_step(j, u):
                t = RING * j + u
                e = pe.value_load(expert[0:1, bass.ds(t, 1)], min_val=0, max_val=EXPERTS - 1)
                if in_loop(t) or t + 1 < SLOT_TILES:
                    up(t + 1, (u + 1) % RING)
                down(t, u, e, range(KF // 2))
                if in_loop(t) or t + 2 < SLOT_TILES:
                    zn_turn(j + (u + 2) // RING, (u + 2) % RING)
                down(t, u, e, range(KF // 2, KF))

            for u in range(RING):
                slot_step(0, u)
            with pe.Fori(*SLOT_RINGS) as j:
                for u in range(RING):
                    slot_step(j, u)
            for t in range(SLOT_RINGS[1] * RING, SLOT_TILES):
                slot_step(t // RING, t % RING)

        @block.vector
        def _(dve):
            def moments(n, s_stat, s_mv, t, pieces, parts=TT):
                for i, piece in enumerate(pieces):
                    ins = nc.vector.bn_stats(stats[0:parts, n, i, :], piece)
                ins.then_inc(s_stat, 1)
                dve.wait_ge(s_stat, t + 1)
                dve.sem_inc(s_passed_dve, 1)
                nc.vector.bn_aggr(mv[0:parts, n, :],
                                  stats[0:parts, n, 0:len(pieces), :].rearrange("p a s -> p (a s)")).then_inc(s_mv, 1)

            def normalise(to, source, n, t, parts=TT):
                dve.wait_ge(s_rstd[n], t + 1)
                return nc.vector.tensor_scalar(to, source, mv[0:parts, n, 0:1], rstd[0:parts, n:n + 1],
                                               ALU.subtract, ALU.mult)

            def x_moments(q, b):
                dve.wait_ge(s_x[b], 16 * (q + 1))
                half = PATCH_DIM // 2
                moments(LN_X, s_xstat, s_xmv, 2 * q + b, [xin[:, b, 0:half], xin[:, b, half:PATCH_DIM]], TP)

            def x_norm(t, b):
                normalise(xin[:, b, :], xin[:, b, :], LN_X, t, TP).then_inc(s_xn, 1)

            def z_moments(t):
                dve.wait_ge(s_zp, t + 1)
                nc.vector.tensor_tensor(z[:, :], p_z, tok_row[:, :], ALU.add).then_inc(s_z, 1)
                dve.wait_ge(s_z, t + 1)
                moments(LN_Z, s_zstat, s_zmv, t, [z[:, :]])

            def h_moments(t):
                normalise(z[:, :], z[:, :], LN_Z, t).then_inc(s_zn, 1)
                dve.wait_ge(s_zn, t + 1)
                nc.vector.tensor_tensor(z[:, :], z[:, :], gain[:, :], ALU.mult).then_inc(s_zg, 1)
                dve.wait_ge(s_zg, t + 1)
                if above_zero(t):
                    dve.wait_ge(s_hb, t)
                nc.vector.tensor_tensor(h[:, :], z[:, :], shift[:, :], ALU.add).then_inc(s_h, 1)
                dve.wait_ge(s_h, t + 1)
                moments(LN_H, s_hstat, s_hmv, t, [h[:, :]])

            def h_norm(t):
                if above_zero(t):
                    dve.wait_ge(s_hTp, t)
                normalise(hn[:, :], h[:, :], LN_H, t).then_inc(s_hn, 1)

            def v_out(t):
                dve.wait_ge(s_vp, t + 1)
                if above_zero(t):
                    dve.wait_ge(s_o, t)
                nc.vector.tensor_tensor(
                    vblk[:, :, :, 0:HEAD_DIM], p_v.rearrange("p (i a d) -> p i a d", i=PER_TILE, a=HEADS),
                    c("head_in_stack", TT).unsqueeze(1).unsqueeze(3).to_broadcast([TT, PER_TILE, HEADS, HEAD_DIM]),
                    ALU.mult).then_inc(s_v, 1)

            def softmax_in(t):
                dve.wait_ge(s_sp, t + 1)
                if above_zero(t):
                    dve.wait_ge(s_pTp, t)
                nc.vector.tensor_tensor(
                    prob[:, :, :].rearrange("p (c a) k -> p c a k", c=KD), p_s.rearrange("p c (a k) -> p c a k", a=HC),
                    c("causal", TT).unsqueeze(1).unsqueeze(1).to_broadcast([TT, KD, HC, T]), ALU.add).then_inc(s_sm, 1)
                dve.wait_ge(s_sm, t + 1)
                nc.vector.tensor_reduce(smax[:, :], prob[:, :, :], AX.X, ALU.max).then_inc(s_smax, 1)
                dve.wait_ge(s_smax, t + 1)
                nc.vector.tensor_tensor(prob[:, :, :], prob[:, :, :],
                                        smax[:, :].unsqueeze(2).to_broadcast([TT, HEADS, T]),
                                        ALU.subtract).then_inc(s_sub, 1)

            def h1_moments(t, b):
                dve.wait_ge(s_o, t + 1)
                o = p_o.rearrange("p (a v) -> p a v", a=HEADS)
                nc.vector.reciprocal(srec[:, :], o[:, :, HEAD_DIM]).then_inc(s_rec, 1)
                dve.wait_ge(s_rec, t + 1)
                if above_zero(t):
                    dve.wait_ge(s_base, t)
                nc.vector.tensor_tensor(h1[:, :].rearrange("p (a d) -> p a d", a=HEADS), o[:, :, 0:HEAD_DIM],
                                        srec[:, :].unsqueeze(2).to_broadcast([TT, HEADS, HEAD_DIM]),
                                        ALU.mult).then_inc(s_on, 1)
                dve.wait_ge(s_on, t + 1)
                dve.wait_ge(s_hb, t + 1)
                nc.vector.tensor_tensor(h1[:, :], h1[:, :], hb[:, b, :], ALU.add).then_inc(s_h1, 1)
                dve.wait_ge(s_h1, t + 1)
                moments(LN_H1, s_h1stat, s_h1mv, t, [h1[:, :]])

            def xn_moments(t):
                if above_zero(t):
                    dve.wait_ge(s_xnTp, t)
                if above_zero(t):
                    dve.wait_ge(s_base, t)
                normalise(xn[:, :], h1[:, :], LN_H1, t).then_inc(s_x2, 1)
                dve.wait_ge(s_x2, t + 1)
                moments(LN_XN, s_x2stat, s_x2mv, t, [xn[:, :]])

            def zn_row(q, b):
                if above_zero(q):
                    dve.wait_ge(s_stored[b], 16 * q)
                normalise(rowbuf[:, b, 0:D], xn[:, :], LN_XN, 2 * q + b).then_inc(s_row, 1)

            def keep_affinity(t):
                dve.wait_ge(s_affp, t + 1)
                nc.vector.tensor_reduce(amax[:, :], p_aff, AX.X, ALU.max).then_inc(s_amax, 1)
                nc.vector.tensor_copy(aff_all[0:TT, bass.ds(t, 1), :].rearrange("p t e -> p (t e)"), p_aff)\
                    .then_inc(s_aff, 1)

            def alpha(t, b):
                dve.wait_ge(s_aexp, t + 1)
                nc.vector.tensor_scalar(ainc[:, :], aexp[:, :], 1.0, None, ALU.add).then_inc(s_ainc, 1)
                dve.wait_ge(s_ainc, t + 1)
                nc.vector.reciprocal(rowbuf[:, b, 2 * D:2 * D + 1], ainc[:, :]).then_inc(s_alpha, 1)

            nc.vector.memset(ones[:], 1.0).then_inc(s_set, 1)
            nc.vector.memset(rowbuf[:, :, 2 * D:ROW], 0.0).then_inc(s_set, 1)
            dve.wait_ge(s_table, 16)
            for i in range(PER_TILE):
                nc.vector.tensor_copy(vblk[:, i, :, HEAD_DIM], c("head_in_stack", TT)).then_inc(s_set, 1)

            dve.wait_ge(s_set, SETS)
            x_moments(0, 0)
            x_norm(0, 0)
            x_moments(0, 1)
            x_norm(1, 1)
            dve.wait_ge(s_rows, 16 * 4)
            nc.vector.tensor_tensor(shift[:, :], shift[:, :], shift2[:, :], ALU.add).then_inc(s_shift, 1)
            dve.wait_ge(s_attn_w, 16 * 4)
            nc.vector.tensor_scalar(bqk_sb[:, 0:KD], bqk_sb[:, 0:KD], float(HEAD_DIM) ** -0.5, None, ALU.mult)\
                .then_inc(s_bq, 1)
            dve.wait_ge(s_shift, 1)
            z_moments(0)
            h_moments(0)
            h_norm(0)
            dve.wait_ge(s_expert_c, 16 * 3)

            def step(q, b):
                t = 2 * q + b
                if exists(q, b, 2):
                    x_moments(*at(q, b, 2))
                    x_norm(t + 2, b)
                if exists(q, b, -2):
                    keep_affinity(t - 2)
                    alpha(t - 2, b)
                if exists(q, b, 1):
                    z_moments(t + 1)
                    h_moments(t + 1)
                if exists(q, b, -1):
                    h1_moments(t - 1, 1 - b)
                if exists(q, b, 1):
                    h_norm(t + 1)
                softmax_in(t)
                if exists(q, b, -1):
                    xn_moments(t - 1)
                v_out(t)
                if exists(q, b, -1):
                    zn_row(*at(q, b, -1))

            step(0, 0)
            step(0, 1)
            step(1, 0)
            with dve.Fori(*PAIRS) as j:
                step(j, 1)
                step(j + 1, 0)
            for t in range(2 * PAIRS[1] + 1, TILES):
                step(t // 2, t % 2)
            end = TILES - 1
            keep_affinity(end - 1)
            alpha(end - 1, 1 - end % 2)
            h1_moments(end, end % 2)
            xn_moments(end)
            zn_row(end // 2, end % 2)
            keep_affinity(end)
            alpha(end, end % 2)

            steps = [0]

            def then(ins):
                steps[0] += 1
                ins.then_inc(r_dve, 1)
                dve.wait_ge(r_dve, steps[0])

            def wide(ap, shape, *axes):
                for a in axes:
                    ap = ap.unsqueeze(a)
                return ap.to_broadcast(shape)

            ET = EXPERTS * TILES
            aff = aff_all[0:TT, :, :]
            te = [TT, TILES, EXPERTS]
            et = [TT, EXPERTS, TILES]
            then(nc.vector.tensor_reduce(r_max[0:TT, :], aff, AX.X, ALU.max))
            then(nc.vector.tensor_tensor(r_val[0:TT], aff, wide(r_max[0:TT, :], te, 2), ALU.is_ge))
            then(nc.vector.tensor_tensor(r_val[0:TT], r_val[0:TT], wide(c("rank", TT), te, 1), ALU.mult))
            then(nc.vector.tensor_reduce(r_first[0:TT, :], r_val[0:TT], AX.X, ALU.max))
            then(nc.vector.tensor_tensor(r_val[0:TT], r_val[0:TT], wide(r_first[0:TT, :], te, 2), ALU.is_equal))
            then(nc.vector.tensor_tensor(onehot[0:TT].rearrange("p e t -> p t e"), r_val[0:TT],
                                         wide(c("live", TT), te, 2), ALU.mult))
            nc.vector.tensor_copy(r_max[0:TT, :], r_max[0:TT, :]).then_inc(s_hot, 1)
            dve.wait_ge(s_count, 1)
            then(nc.vector.tensor_copy(tot[:, :, :].rearrange("p e t -> p (e t)"), p_count[:, ET:2 * ET]))
            then(nc.vector.tensor_tensor_scan(through[:, :, :].rearrange("p e t -> p (e t)"), c("restart"),
                                              tot[:, :, :].rearrange("p e t -> p (e t)"), 0.0, ALU.mult, ALU.add))
            shape = [P, EXPERTS, TOKENS // P + 1]
            then(nc.vector.tensor_tensor(r_cmp[:, :, :], through[:, :, TILES - 1].unsqueeze(2).to_broadcast(shape),
                                         wide(c("gt_slots"), shape, 1), ALU.is_gt))
            then(nc.vector.tensor_reduce(n_tiles[:, :], r_cmp[:, :, :], AX.X, ALU.add))
            then(nc.vector.tensor_tensor_scan(tile_end[:, :], ones[:, 0:EXPERTS], n_tiles[:, :], 0.0,
                                              ALU.mult, ALU.add))
            then(nc.vector.tensor_tensor(tile_start[:, :], tile_end[:, :], n_tiles[:, :], ALU.subtract))
            then(nc.vector.tensor_scalar(tile_start[:, :], tile_start[:, :], float(P), None, ALU.mult))
            then(nc.vector.tensor_tensor(place[0:TT], through[0:TT], tot[0:TT], ALU.subtract))
            then(nc.vector.tensor_tensor(place[0:TT], place[0:TT], wide(tile_start[0:TT, :], et, 2), ALU.add))
            then(nc.vector.tensor_tensor(place[0:TT], place[0:TT],
                                         p_count[0:TT, 0:ET].rearrange("p (e t) -> p e t", e=EXPERTS), ALU.add))
            then(nc.vector.tensor_tensor(place[0:TT], place[0:TT], onehot[0:TT], ALU.mult))
            then(nc.vector.tensor_reduce(pos[0:TT, :], place[0:TT].rearrange("p e t -> p t e"), AX.X, ALU.add))
            shape = [TT, TILES, SLOT_TILES - 1]
            then(nc.vector.tensor_tensor(r_ge[0:TT], wide(pos[0:TT, :], shape, 2), wide(c("ge_slots", TT), shape, 1),
                                         ALU.is_ge))
            then(nc.vector.tensor_reduce(slot_tile[0:TT, :], r_ge[0:TT], AX.X, ALU.add))
            then(nc.vector.scalar_tensor_tensor(slot_row[0:TT, :], slot_tile[0:TT, :], -float(P), pos[0:TT, :],
                                                ALU.mult, ALU.add))
            shape = [TT, TILES, SLOT_TILES]
            then(nc.vector.tensor_tensor(tile_hot[0:TT], wide(slot_tile[0:TT, :], shape, 2),
                                         wide(c("tile_no", TT), shape, 1), ALU.is_equal))
            then(nc.vector.tensor_tensor(tile_hot[0:TT], tile_hot[0:TT], wide(c("token", TT), shape, 2), ALU.mult))
            for t in range(TILES):
                ins = nc.vector.tensor_scalar(row_hot[0:TT, t, :], c("iota", TT), slot_row[0:TT, t:t + 1], None,
                                              ALU.is_equal)
            ins.then_inc(s_rowhot, 1)
            shape = [P, SLOT_TILES, EXPERTS]
            then(nc.vector.tensor_tensor(e_cmp[:, :, :], wide(c("tile_no"), shape, 2), wide(tile_end[:, :], shape, 1),
                                         ALU.is_ge))
            then(nc.vector.tensor_reduce(e_sum[:, :], e_cmp[:, :, :], AX.X, ALU.add))
            then(nc.vector.tensor_scalar(expert[:, :], e_sum[:, :], EXPERTS - 1.0, None, ALU.min))
            dve.wait_ge(s_slotp, 1)
            then(nc.vector.tensor_copy(slot[:, :], p_slot))
            then(nc.vector.tensor_scalar(gather_all[:, :], slot[:, :], 1.0, 0.0, ALU.subtract, ALU.max))
            then(nc.vector.tensor_scalar(empty[:, :], slot[:, :], 0.5, NO_TOKEN, ALU.is_lt, ALU.mult))
            then(nc.vector.tensor_scalar(slot_m1[:, :], slot[:, :], 1.0, None, ALU.subtract))
            then(nc.vector.tensor_tensor(scatter_all[:, :], slot_m1[:, :], empty[:, :], ALU.add))
            nc.vector.tensor_copy(slot_m1[:, :], slot_m1[:, :]).then_inc(s_route, 1)

            def columns(j, u):
                t = RING * j + u
                e = dve.value_load(expert[0:1, bass.ds(t, 1)], min_val=0, max_val=EXPERTS - 1)
                if above_zero(t - RING + 1):
                    dve.wait_ge(s_relu, KF * (t - RING + 1))
                nc.vector.tensor_copy(cur[:, u, :], cols_sb[:, bass.ds(e, 1), :].rearrange("p e n -> p (e n)"))\
                    .then_inc(s_cur, 1)
                nc.vector.tensor_copy(b2_cur[:, u, :], b2_sb[:, bass.ds(e, 1), :].rearrange("p e n -> p (e n)"))\
                    .then_inc(s_b2cur, 1)
                nc.vector.tensor_copy(w1_cur[:, u, :, :].rearrange("p c n -> p (c n)"),
                                      w1_sb[:, bass.ds(e, 1), :, :].rearrange("p e c n -> p (e c n)"))\
                    .then_inc(s_w1cur, 1)

            def z_out(t, u):
                dve.wait_ge(s_zTp, t + 1)
                dve.wait_ge(s_cur, t + 1)
                if above_zero(t):
                    dve.wait_ge(s_up, KF * t)
                for k in range(KD):
                    ins = nc.vector.tensor_scalar(zT[:, k, :], p_zT[:, k * P:(k + 1) * P], cur[:, u, k:k + 1],
                                                  cur[:, u, KD + k:KD + k + 1], ALU.mult, ALU.add)
                ins.then_inc(s_zTe, 1)

            def finish(j, u):
                t = RING * j + u
                dve.wait_ge(s_down, t + 1)
                dve.wait_ge(s_b2cur, t + 1)
                if above_zero(t):
                    dve.wait_ge(s_y, t)
                nc.vector.tensor_tensor(y1[:, :], p_down, b2_cur[:, u, :], ALU.add).then_inc(s_y1, 1)
                dve.wait_ge(s_y1, t + 1)
                dve.wait_ge(s_gather[u], 16 * (j + 1))
                if above_zero(16 * j):
                    dve.wait_ge(s_scatter[u], 16 * j)
                nc.vector.scalar_tensor_tensor(yout[:, u, :], y1[:, :], rows[:, u, 2 * D:2 * D + 1],
                                               rows[:, u, D:2 * D], ALU.mult, ALU.add).then_inc(s_y, 1)

            dve.wait_ge(s_w, 16 * 2 * EXPERTS)
            columns(0, 0)
            z_out(0, 0)
            columns(0, 1)
            z_out(1, 1)
            columns(0, 2)

            def slot_step(j, u):
                t = RING * j + u
                if in_loop(t) or t + 2 < SLOT_TILES:
                    z_out(t + 2, (u + 2) % RING)
                finish(j, u)
                if in_loop(t) or t + RING < SLOT_TILES:
                    columns(j + 1, u)

            for u in range(RING):
                slot_step(0, u)
            with dve.Fori(*SLOT_RINGS) as j:
                for u in range(RING):
                    slot_step(j, u)
            for t in range(SLOT_RINGS[1] * RING, SLOT_TILES):
                slot_step(t // RING, t % RING)


def _table():
    t = np.zeros((P, TABLE), np.float32)
    p = np.arange(P)[:, None]

    def put(name, value):
        a, w = COLS[name]
        t[:, a:a + w] = value

    put("ident", p == np.arange(P))
    put("before", p < np.arange(P))
    put("iota", np.arange(P))
    put("head_of_row", p // HEAD_DIM == np.arange(HC))
    put("head_in_stack", p // T == np.arange(HEADS) % PER_TILE)
    put("causal", np.where(np.arange(T) <= p % T, 0.0, MASKED))
    token = np.arange(TILES) * TT + p
    put("token", (token + 1) * (token < TOKENS))
    put("live", token < TOKENS)
    put("ge_slots", P * np.arange(1, SLOT_TILES))
    put("gt_slots", P * np.arange(TOKENS // P + 1))
    put("tile_no", np.arange(SLOT_TILES))
    put("rank", EXPERTS - np.arange(EXPERTS))
    put("restart", np.tile(np.arange(TILES) > 0, EXPERTS))
    return t


def _positions():
    ys, xs = np.meshgrid(np.arange(GRID), np.arange(GRID), indexing="ij")
    omega = np.arange(D // 4, dtype=np.float32) / np.float32(D // 4 - 1)
    omega = (np.float32(1.0) / np.float32(TEMPERATURE) ** omega).astype(np.float32)
    ys = ys.reshape(-1)[:, None].astype(np.float32) * omega
    xs = xs.reshape(-1)[:, None].astype(np.float32) * omega
    return np.concatenate([np.sin(xs), np.cos(xs), np.sin(ys), np.cos(ys)], axis=1).astype(np.float32)


def _chunks(a):
    return np.ascontiguousarray(a.reshape(-1, P, a.shape[-1]).transpose(1, 0, 2).reshape(P, -1))


def kernel(x, cls_tok, L0_tok_cls_token, L0_tok_cls_pos_embedding, L0_tok_ln1_g, L0_tok_ln1_b, L0_tok_W,
           L0_tok_bias, L0_tok_ln2_g, L0_tok_ln2_b, L0_attn_W, L0_attn_b, L0_ffn_centroids, L0_ffn_ln_g,
           L0_ffn_ln_b, L0_ffn_w1, L0_ffn_b1, L0_ffn_w2, L0_ffn_b2):
    import concourse.bacc as bacc
    from concourse.bass_utils import run_bass_kernel_spmd

    x = np.asarray(x).reshape(IMAGES, CHANNELS, GRID, PATCH, GRID, PATCH)
    patches = x.transpose(0, 2, 4, 3, 5, 1).reshape(IMAGES * PATCHES, PATCH_DIM)

    def row(a):
        return np.asarray(a).reshape(1, -1)

    def image_rows(first, second, patch):
        patch = np.broadcast_to(patch, (PATCHES, D))
        return np.tile(np.concatenate([first, second, patch]), (PER_TILE, 1))

    none = np.zeros((1, D), np.float32)
    attn_w = np.asarray(L0_attn_W)
    attn_b = np.asarray(L0_attn_b)
    cols = np.concatenate([np.asarray(a).reshape(EXPERTS, -1, P) for a in (L0_ffn_ln_g, L0_ffn_ln_b, L0_ffn_b1)],
                          axis=1)
    w1 = np.asarray(L0_ffn_w1).transpose(0, 2, 1).reshape(EXPERTS, KD, P, HIDDEN).transpose(0, 2, 1, 3)
    w2 = np.asarray(L0_ffn_w2).transpose(0, 2, 1).reshape(EXPERTS, KF, P, D).transpose(0, 2, 1, 3)
    inputs = {
        "x": patches,
        "tok_add": image_rows(row(cls_tok), row(L0_tok_cls_token), row(L0_tok_ln2_b)),
        "tok_add2": image_rows(none, row(L0_tok_cls_pos_embedding), _positions()),
        "tok_gain": image_rows(none, none, row(L0_tok_ln2_g)),
        "ln1_gb": np.concatenate([np.asarray(L0_tok_ln1_g), np.asarray(L0_tok_ln1_b)]).reshape(2 * KX, P).T,
        "tok_w": _chunks(np.asarray(L0_tok_W)),
        "tok_bias": np.asarray(L0_tok_bias).reshape(D),
        "wqk": _chunks(attn_w[0:2 * D].T),
        "wv": _chunks(attn_w[2 * D:].T),
        "bqk": attn_b[0:2 * D].reshape(2 * KD, P).T,
        "bv": attn_b[2 * D:],
        "centroids": _chunks(np.asarray(L0_ffn_centroids).T),
        "expert_cols": cols.transpose(2, 0, 1).reshape(P, -1),
        "expert_b2": np.asarray(L0_ffn_b2).reshape(-1),
        "w1": w1.reshape(EXPERTS * P, -1),
        "w2": w2.reshape(EXPERTS * P, -1),
        "table": _table(),
    }
    nc = bacc.Bacc("TRN2", target_bir_lowering=False, num_devices=1)
    arrays, aps = {}, {}
    for name, a in inputs.items():
        a = np.ascontiguousarray(a)
        arrays[f"in_{name}"] = a
        aps[name] = nc.dram_tensor(f"in_{name}", a.shape, mybir.dt.from_np(a.dtype), kind="ExternalInput").ap()
    out = nc.dram_tensor("out", (TOKENS, D), F32, kind="ExternalOutput").ap()
    attention_tower(nc, out=out, **aps)
    r = run_bass_kernel_spmd(nc, [arrays], core_ids=[0])
    return r.results[0]["out"].reshape(IMAGES, T, D)
```

```python
from contextlib import ExitStack

import numpy as np

import concourse.bass as bass
from concourse import mybir

F32 = mybir.dt.float32
F16 = mybir.dt.float16
I32 = mybir.dt.int32
ALU = mybir.AluOpType
ACT = mybir.ActivationFunctionType
AX = mybir.AxisListType

IMAGES, CHANNELS, SIDE, PATCH = 32, 3, 96, 16
GRID = SIDE // PATCH
PATCHES = GRID * GRID
PATCH_DIM = CHANNELS * PATCH * PATCH
D = 256
HEADS, HEAD_DIM = 16, 16
EXPERTS, HIDDEN = 8, 1024
EPS = 1e-5
TEMPERATURE = 10000.0
P = 128

T = PATCHES + 2
PER_TILE = 3
TT = PER_TILE * T
TP = PER_TILE * PATCHES
TILES = -(-IMAGES // PER_TILE)
LAST_IMAGES = IMAGES - (TILES - 1) * PER_TILE
TOKENS = IMAGES * T
KX = PATCH_DIM // P
KD = D // P
KF = HIDDEN // P
HC = P // HEAD_DIM
GROUPS = -(-HEADS // PER_TILE)
VW = HEAD_DIM + 1
MASKED = -1e30

SLOT_TILES = (TOKENS - EXPERTS) // P + EXPERTS
ROW = 2 * D + 8
NO_TOKEN = 4096.0
RING = 3

_WIDTHS = [("ident", P), ("before", P), ("iota", P), ("head_of_row", HC), ("head_in_stack", HEADS),
           ("causal", T), ("token", TILES), ("live", TILES), ("ge_slots", SLOT_TILES - 1),
           ("gt_slots", TOKENS // P + 1), ("tile_no", SLOT_TILES), ("rank", EXPERTS),
           ("restart", EXPERTS * TILES)]
COLS = {}
_at = 0
for _name, _width in _WIDTHS:
    COLS[_name] = (_at, _width)
    _at += _width
TABLE = _at


def attention_tower(nc, x, tok_add, tok_add2, tok_gain, ln1_gb, tok_w, tok_bias, wqk, wv, bqk, bv,
                    centroids, expert_cols, expert_b2, w1, w2, table, out):
    rows_dram = nc.dram_tensor("token_rows", (TOKENS, ROW), F32)
    values_dram = nc.dram_tensor("value_rows", (TILES * TT, D), F32)
    with ExitStack() as ctx:
        def sb(name, shape, dt=F32):
            return ctx.enter_context(nc.sbuf_tensor(name, shape, dt))

        def sem(name):
            return ctx.enter_context(nc.semaphore(name))

        tab = sb("tab", [P, TABLE])
        ones = sb("ones", [P, P])
        w1_sb = sb("w1_sb", [P, EXPERTS, KD, HIDDEN])
        w2_sb = sb("w2_sb", [P, EXPERTS, KF, D])
        cols_sb = sb("cols_sb", [P, EXPERTS, 2 * KD + KF])
        cent_sb = sb("cent_sb", [P, KD, EXPERTS])
        aff_all = sb("aff_all", [P, TILES, EXPERTS])

        phase_a = ExitStack()

        def sa(name, shape, dt=F32):
            return phase_a.enter_context(nc.sbuf_tensor(name, shape, dt))

        tokw = sa("tokw", [P, KX, D])
        tok_row = sa("tok_row", [TT, D])
        gain = sa("gain", [TT, D])
        shift = sa("shift", [TT, D])
        ln1 = sa("ln1", [P, 2, KX])
        wqk_sb = sa("wqk_sb", [P, KD, 2 * D])
        wv_sb = sa("wv_sb", [P, KD, D])
        bqk_sb = sa("bqk_sb", [P, 4])
        bv_sb = sa("bv_sb", [TT, D])
        xin = sa("xin", [TP, 2, PATCH_DIM])
        xT = sa("xT", [P, KX, TT])
        z = sa("z", [TT, D])
        h = sa("h", [TT, D])
        hb = sa("hb", [TT, 2, D])
        hn = sa("hn", [TT, D])
        hT = sa("hT", [P, KD, TT])
        qT = sa("qT", [P, KD, PER_TILE * (TT + T)])
        kT = sa("kT", [P, KD, TT])
        kblk = sa("kblk", [P, KD, PER_TILE, HC, T])
        values = sa("values", [TT, D])
        vstack = sa("vstack", [TT, PER_TILE, D])
        vblk = sa("vblk", [TT, PER_TILE, HEADS, VW])
        prob = sa("prob", [TT, HEADS, T])
        probT = sa("probT", [TT, GROUPS, PER_TILE * (TT + T)])
        h1 = sa("h1", [TT, D])
        shift2 = h1
        xn = sa("xn", [TT, D])
        xnT = sa("xnT", [P, KD, TT])
        stats = sa("stats", [TT, 5, 2, 6])
        mv = sa("mv", [TT, 5, 2])
        eps_col = sa("eps_col", [TT, 1])
        half_col = sa("half_col", [TT, 1])
        var_eps = sa("var_eps", [TT, 5])
        rstd = sa("rstd", [TT, 5])
        smax = sa("smax", [TT, HEADS])
        srec = sa("srec", [TT, HEADS])
        amax = sa("amax", [TT, 1])
        aexp = sa("aexp", [TT, 1])
        ainc = sa("ainc", [TT, 1])
        rowbuf = sa("rowbuf", [TT, 2, ROW])
        phase_a.close()

        b2_sb = sb("b2_sb", [P, EXPERTS, D])
        onehot = sb("onehot", [P, EXPERTS, TILES])
        r_max = sb("r_max", [P, TILES])
        r_val = sb("r_val", [P, TILES, EXPERTS])
        r_first = sb("r_first", [P, TILES])
        through = sb("through", [P, EXPERTS, TILES])
        tot = sb("tot", [P, EXPERTS, TILES])
        r_cmp = sb("r_cmp", [P, EXPERTS, TOKENS // P + 1])
        n_tiles = sb("n_tiles", [P, EXPERTS])
        tile_end = sb("tile_end", [P, EXPERTS])
        tile_start = sb("tile_start", [P, EXPERTS])
        place = sb("place", [P, EXPERTS, TILES])
        pos = sb("pos", [P, TILES])
        r_ge = sb("r_ge", [P, TILES, SLOT_TILES - 1])
        tile_hot = sb("tile_hot", [P, TILES, SLOT_TILES])
        slot_tile = sb("slot_tile", [P, TILES])
        slot_row = sb("slot_row", [P, TILES])
        tile_token = sb("tile_token", [P, TILES, SLOT_TILES], F16)
        row_hot = sb("row_hot", [P, TILES, P], F16)
        empty = sb("empty", [P, SLOT_TILES])
        gather_all = sb("gather_all", [P, SLOT_TILES], I32)
        scatter_all = sb("scatter_all", [P, SLOT_TILES], I32)
        e_cmp = sb("e_cmp", [P, SLOT_TILES, EXPERTS])
        e_sum = sb("e_sum", [P, SLOT_TILES])
        expert = sb("expert", [P, SLOT_TILES], I32)

        cur = sb("cur", [P, RING, 2 * KD + KF])
        rows = sb("rows", [P, RING, ROW])
        zT = sb("zT", [P, RING, KD, P])
        w1_cur = sb("w1_cur", [P, RING, KD, HIDDEN])
        b2_cur = sb("b2_cur", [P, RING, D])
        hidT = sb("hidT", [P, RING, KF, P])
        y1 = sb("y1", [P, D])
        yout = sb("yout", [P, RING, D])

        ps = ctx.enter_context(nc.psum_tensor("ps", [P, 8, 512], F32))

        def c(name, n=P):
            a, w = COLS[name]
            return tab[0:n, a:a + w]

        ident = c("ident")

        def bank(n, width, parts=P, banks=1):
            return ps[0:parts, n:n + banks, :].rearrange("p b n -> p (b n)")[:, 0:width]

        p_xT = ps[:, 0:2, 0:3 * TP]
        p_z = bank(2, D, TT)
        p_hT = bank(3, KD * TT)
        p_v = ps[0:TT, 3, KD * TT:KD * TT + D]
        p_qk = bank(4, 4 * TT)
        p_o = bank(5, HEADS * VW, TT)
        p_aff = ps[0:TT, 4, 4 * TT:4 * TT + EXPERTS]
        p_xnT = ps[:, 5, HEADS * VW:HEADS * VW + KD * TT]
        p_s = ps[0:TT, 6:8, 0:HC * T]
        p_pT = [ps[0:TT, 6, 0:4 * TT], ps[0:TT, 7, 0:2 * TT]]
        p_count = bank(2, 2 * EXPERTS * TILES)
        p_slot = bank(4, SLOT_TILES)
        p_zT = bank(0, KD * P)
        p_hidT = bank(1, KF * P, P, 2)
        p_down = bank(7, D)
        p_down_last = bank(3, D)

        s_table = sem("table_loaded")
        s_embed_w = sem("embedding_weights_loaded")
        s_rows = sem("token_rows_loaded")
        s_attn_w = sem("attention_weights_loaded")
        s_expert_c = sem("expert_consts_loaded")
        s_b2 = sem("expert_b2_loaded")
        s_w = sem("experts_loaded")
        s_set = sem("buffers_set")
        s_bq = sem("query_bias_scaled")
        s_shift = sem("shift_ready")
        s_x = [sem("x_loaded_even"), sem("x_loaded_odd")]
        s_xstat = sem("x_stats")
        s_xmv = sem("x_moments")
        s_xn = sem("x_normalised")
        s_xTp = sem("x_halves_transposed")
        s_xT = sem("xT_chunks_ready")
        s_zp = sem("z_summed")
        s_z = sem("z_ready")
        s_zstat = sem("z_stats")
        s_zmv = sem("z_moments")
        s_zn = sem("z_normalised")
        s_zg = sem("z_scaled")
        s_h = sem("h_ready")
        s_hstat = sem("h_stats")
        s_hmv = sem("h_moments")
        s_hn = sem("h_normalised")
        s_hb = sem("h_plus_bv")
        s_hTp = sem("h_transposed")
        s_hT = sem("hT_ready")
        s_qkp = sem("qk_projected")
        s_q = sem("q_ready")
        s_k = sem("k_ready")
        s_kblk = sem("k_blocks_ready")
        s_vp = sem("v_projected")
        s_values = sem("values_kept")
        s_vput = sem("values_in_dram")
        s_vstack = sem("values_stacked")
        s_v = sem("v_blocks_ready")
        s_sp = sem("scores_summed")
        s_sm = sem("scores_masked")
        s_smax = sem("score_max")
        s_sub = sem("scores_shifted")
        s_exp = sem("exp_done")
        s_pTp = sem("probs_transposed")
        s_pT = sem("probT_ready")
        s_o = sem("attention_summed")
        s_rec = sem("sums_inverted")
        s_on = sem("attention_scaled")
        s_h1 = sem("h1_ready")
        s_h1stat = sem("h1_stats")
        s_h1mv = sem("h1_moments")
        s_x2 = sem("xn_ready")
        s_base = sem("base_ready")
        s_x2stat = sem("xn_stats")
        s_x2mv = sem("xn_moments")
        s_row = sem("row_zn_ready")
        s_xnTp = sem("xn_transposed")
        s_xnT = sem("xnT_ready")
        s_affp = sem("affinity_summed")
        s_aff = sem("affinity_kept")
        s_amax = sem("affinity_max")
        s_aexp = sem("alpha_exp")
        s_ainc = sem("alpha_plus_one")
        s_alpha = sem("alpha_ready")
        s_stored = [sem("rows_stored_even"), sem("rows_stored_odd")]
        s_var = [sem(f"variance_eps_{n}") for n in range(5)]
        s_rstd = [sem(f"rstd_{n}") for n in range(5)]

        s_passed_dve = sem("waits_passed_vector")
        SETS = 5 + 2 + PER_TILE
        LN_X, LN_Z, LN_H, LN_H1, LN_XN = range(5)

        def in_loop(t):
            return not isinstance(t, int)

        def above_zero(count):
            return in_loop(count) or count > 0

        def at(q, b, k):
            return q + (b + k) // 2, (b + k) % 2

        def exists(q, b, k=0):
            return in_loop(q) or 0 <= 2 * q + b + k < TILES

        def last(t):
            return not in_loop(t) and t == TILES - 1

        PAIRS = (1, (TILES - 3) // 2)
        SLOT_RINGS = (1, (SLOT_TILES - RING) // RING)

        r_dve = sem("routing_step")
        s_hot = sem("onehot_ready")
        s_count = sem("counts_summed")
        s_rowhot = sem("slot_hots_ready")
        s_slotp = sem("slots_summed")
        s_route = sem("gather_indices_ready")
        s_expert = sem("tile_experts_ready")
        s_gather = [sem(f"rows_gathered_{n}") for n in range(RING)]
        s_scatter = [sem(f"rows_scattered_{n}") for n in range(RING)]
        s_cur = sem("expert_columns_ready")
        s_zTp = sem("zn_transposed")
        s_zTe = sem("zT_ready")
        s_w1cur = sem("expert_w1_ready")
        s_b2cur = sem("expert_b2_ready")
        s_up = sem("up_summed")
        s_relu = sem("hidden_relu")
        s_down = sem("down_summed")
        s_y1 = sem("y_plus_b2")
        s_y = sem("y_ready")

        block = ctx.enter_context(nc.Block())

        @block.sync
        def _(sp):
            def load_x(q, b):
                t = 2 * q + b
                if above_zero(t - 1):
                    sp.wait_ge(s_xTp, 2 * (t - 1))
                n = LAST_IMAGES * PATCHES if last(t) else TP
                sp.dma_start(xin[0:n, b, :], x[bass.ds(t * TP, n), :]).then_inc(s_x[b], 16)

            def stack_values(q, b):
                t = 2 * q + b
                tile_rows = values_dram[bass.ds(t * TT, TT), :]
                sp.wait_ge(s_values, t + 1)
                sp.dma_start(tile_rows, values[:, :]).then_inc(s_vput, 16)
                sp.wait_ge(s_vput, 16 * (t + 1))
                if above_zero(t):
                    sp.wait_ge(s_v, t)
                for r in range(PER_TILE):
                    sp.dma_start(vstack[r * T:(r + 1) * T, :, :],
                                 tile_rows.rearrange("(i k) d -> k i d", i=PER_TILE)).then_inc(s_vstack, 16)

            def store_rows(q, b):
                t = 2 * q + b
                sp.wait_ge(s_row, t + 1)
                sp.wait_ge(s_base, t + 1)
                sp.wait_ge(s_alpha, t + 1)
                n = LAST_IMAGES * T if last(t) else TT
                sp.dma_start(rows_dram[bass.ds(t * TT, n), :], rowbuf[0:n, b, :]).then_inc(s_stored[b], 16)

            def step(q, b):
                stack_values(q, b)
                if exists(q, b, 3):
                    load_x(*at(q, b, 3))
                if exists(q, b, -2):
                    store_rows(*at(q, b, -2))

            load_x(0, 0)
            sp.dma_start(tok_row[:, :], tok_bias.partition_broadcast(TT)).then_inc(s_rows, 16)
            sp.dma_start(gain[:, :], tok_gain).then_inc(s_rows, 16)
            sp.dma_start(shift[:, :], tok_add).then_inc(s_rows, 16)
            sp.dma_start(shift2[:, :], tok_add2).then_inc(s_rows, 16)
            load_x(0, 1)
            sp.dma_start(wqk_sb[:, :, :].rearrange("p c n -> p (c n)"), wqk).then_inc(s_attn_w, 16)
            sp.dma_start(bqk_sb[:, :], bqk).then_inc(s_attn_w, 16)
            sp.dma_start(wv_sb[:, :, :].rearrange("p c n -> p (c n)"), wv).then_inc(s_attn_w, 16)
            sp.dma_start(bv_sb[:, :], bv.partition_broadcast(TT)).then_inc(s_attn_w, 16)
            load_x(1, 0)
            sp.dma_start(cent_sb[:, :, :].rearrange("p c n -> p (c n)"), centroids).then_inc(s_expert_c, 16)
            sp.dma_start(cols_sb[:, :, :].rearrange("p e n -> p (e n)"), expert_cols).then_inc(s_expert_c, 16)
            step(0, 0)
            step(0, 1)
            step(1, 0)
            with sp.Fori(PAIRS[0], PAIRS[1] - 1) as j:
                step(j, 1)
                step(j + 1, 0)
            for t in range(2 * PAIRS[1] - 1, TILES):
                step(t // 2, t % 2)
            sp.wait_ge(s_zp, TILES)
            sp.wait_ge(s_zg, TILES)
            sp.dma_start(b2_sb[:, :, :].rearrange("p e n -> p (e n)"), expert_b2.partition_broadcast(P)).then_inc(s_b2, 16)
            for t in (TILES - 2, TILES - 1):
                store_rows(t // 2, t % 2)

        @block.gpsimd
        def _(pool):
            def inv_std(n, moments, t, parts=TT):
                pool.wait_ge(moments, t + 1)
                nc.gpsimd.tensor_tensor(var_eps[0:parts, n:n + 1], mv[0:parts, n, 1:2], eps_col[0:parts, :],
                                        ALU.add).then_inc(s_var[n], 1)
                pool.wait_ge(s_var[n], t + 1)
                nc.gpsimd.tensor_tensor(rstd[0:parts, n:n + 1], var_eps[0:parts, n:n + 1], half_col[0:parts, :],
                                        ALU.pow).then_inc(s_rstd[n], 1)

            def key_blocks(q, b, ch):
                t = 2 * q + b
                pool.wait_ge(s_k, t + 1)
                if above_zero(t):
                    pool.wait_ge(s_sp, t)
                for i in range(LAST_IMAGES if last(t) else PER_TILE):
                    ins = nc.gpsimd.tensor_tensor(
                        kblk[:, ch, i, :, :],
                        kT[:, ch, i * T:(i + 1) * T].unsqueeze(1).to_broadcast([P, HC, T]),
                        c("head_of_row").unsqueeze(2).to_broadcast([P, HC, T]), ALU.mult)
                ins.then_inc(s_kblk, 1)

            def base(q, b):
                pool.wait_ge(s_x2, 2 * q + b + 1)
                if above_zero(q):
                    pool.wait_ge(s_stored[b], 16 * q)
                nc.gpsimd.tensor_tensor(rowbuf[:, b, D:2 * D], h1[:, :], xn[:, :], ALU.add).then_inc(s_base, 1)

            def value_bias(q, b):
                t = 2 * q + b
                pool.wait_ge(s_h, t + 1)
                if above_zero(t - 1):
                    pool.wait_ge(s_h1, t - 1)
                nc.gpsimd.tensor_tensor(hb[:, b, :], h[:, :], bv_sb[:, :], ALU.add).then_inc(s_hb, 1)

            def value_blocks(q, b):
                t = 2 * q + b
                pool.wait_ge(s_vstack, 16 * PER_TILE * (t + 1))
                if above_zero(t):
                    pool.wait_ge(s_o, t)
                nc.gpsimd.tensor_tensor(
                    vblk[:, :, :, 0:HEAD_DIM], vstack[:, :, :].rearrange("p i (a d) -> p i a d", a=HEADS),
                    c("head_in_stack", TT).unsqueeze(1).unsqueeze(3).to_broadcast([TT, PER_TILE, HEADS, HEAD_DIM]),
                    ALU.mult).then_inc(s_v, 1)

            nc.gpsimd.memset(eps_col[:], EPS).then_inc(s_set, 1)
            nc.gpsimd.memset(half_col[:], -0.5).then_inc(s_set, 1)
            nc.gpsimd.memset(xT[:], 0.0).then_inc(s_set, 1)
            nc.gpsimd.memset(qT[:], 0.0).then_inc(s_set, 1)
            nc.gpsimd.memset(probT[:], 0.0).then_inc(s_set, 1)
            pool.wait_ge(s_set, SETS)

            inv_std(LN_X, s_xmv, 0, TP)
            inv_std(LN_X, s_xmv, 1, TP)
            inv_std(LN_Z, s_zmv, 0)
            inv_std(LN_H, s_hmv, 0)
            pool.wait_ge(s_table, 16)
            pool.wait_ge(s_attn_w, 16 * 4)
            value_bias(0, 0)
            inv_std(LN_Z, s_zmv, 1)

            def step(q, b):
                t = 2 * q + b
                key_blocks(q, b, 0)
                if exists(q, b, 2):
                    inv_std(LN_X, s_xmv, t + 2, TP)
                if exists(q, b, 1):
                    inv_std(LN_H, s_hmv, t + 1)
                key_blocks(q, b, 1)
                if exists(q, b, 1):
                    value_bias(*at(q, b, 1))
                if last(t):
                    inv_std(LN_XN, s_x2mv, t - 2)
                    base(*at(q, b, -2))
                    value_blocks(q, b)
                if exists(q, b, -1):
                    inv_std(LN_H1, s_h1mv, t - 1)
                if not last(t):
                    value_blocks(q, b)
                if exists(q, b, -1) and (in_loop(t) or t != TILES - 2):
                    inv_std(LN_XN, s_x2mv, t - 1)
                    base(*at(q, b, -1))
                if exists(q, b, 2):
                    inv_std(LN_Z, s_zmv, t + 2)

            step(0, 0)
            step(0, 1)
            step(1, 0)
            with pool.Fori(*PAIRS) as j:
                step(j, 1)
                step(j + 1, 0)
            for t in range(2 * PAIRS[1] + 1, TILES):
                step(t // 2, t % 2)
            inv_std(LN_H1, s_h1mv, TILES - 1)
            inv_std(LN_XN, s_x2mv, TILES - 1)
            base((TILES - 1) // 2, (TILES - 1) % 2)

            pool.wait_ge(s_stored[0], 16 * -(-TILES // 2))
            pool.wait_ge(s_stored[1], 16 * (TILES // 2))

            def gather(t):
                if above_zero(t - RING + 1):
                    pool.wait_ge(s_y, t - RING + 1)
                nc.gpsimd.indirect_dma_start(
                    rows[:, t % RING, :], None, rows_dram[:, :],
                    bass.IndirectOffsetOnAxis(ap=gather_all[:, t:t + 1], axis=0)).then_inc(s_gather[t % RING], 16)

            pool.wait_ge(s_route, 1)
            for t in range(RING):
                gather(t)
            pool.wait_ge(s_expert, 1)
            for t in range(SLOT_TILES):
                if t + RING < SLOT_TILES:
                    gather(t + RING)
                pool.wait_ge(s_y, t + 1)
                nc.gpsimd.indirect_dma_start(
                    out, bass.IndirectOffsetOnAxis(ap=scatter_all[:, t:t + 1], axis=0), yout[:, t % RING, :], None,
                    bounds_check=TOKENS - 1, oob_is_err=False).then_inc(s_scatter[t % RING], 16)
            for u in range(RING):
                pool.wait_ge(s_scatter[u], 16 * len(range(u, SLOT_TILES, RING)))

        @block.scalar
        def _(act):
            act.dma_start(tab[:, :], table).then_inc(s_table, 16)
            act.dma_start(tokw[:, :, :].rearrange("p c n -> p (c n)"), tok_w).then_inc(s_embed_w, 16)
            act.dma_start(ln1[:, :, :].rearrange("p a c -> p (a c)"), ln1_gb).then_inc(s_embed_w, 16)

            def x_out(t):
                if above_zero(t):
                    act.wait_ge(s_zp, t)
                for k in range(KX):
                    if k % 3 == 0:
                        act.wait_ge(s_xTp, 2 * t + k // 3 + 1)
                    nc.scalar.activation(
                        xT[:, k, :].rearrange("p (i k) -> p i k", i=PER_TILE)[:, :, 2:T],
                        p_xT[:, k // 3, (k % 3) * TP:(k % 3 + 1) * TP].rearrange("p (i k) -> p i k", i=PER_TILE),
                        ACT.Identity, bias=ln1[:, 1, k:k + 1], scale=ln1[:, 0, k:k + 1]).then_inc(s_xT, 1)

            def h_out(t):
                act.wait_ge(s_hTp, t + 1)
                if above_zero(t):
                    act.wait_ge(s_vp, t)
                ins = nc.scalar.activation(hT[:, :, :].rearrange("p c n -> p (c n)"), p_hT, ACT.Copy)
                ins.then_inc(s_hT, 1)

            def k_out(t):
                act.wait_ge(s_qkp, t + 1)
                if above_zero(t):
                    act.wait_ge(s_kblk, KD * t)
                for ch in range(KD):
                    ins = nc.scalar.activation(kT[:, ch, :], p_qk[:, (KD + ch) * TT:(KD + ch + 1) * TT],
                                               ACT.Identity, bias=bqk_sb[:, KD + ch:KD + ch + 1])
                ins.then_inc(s_k, 1)

            def q_out(t):
                if above_zero(t):
                    act.wait_ge(s_sp, t)
                blocks = qT[:, :, :].rearrange("p c (i s) -> p c i s", i=PER_TILE)[:, :, :, 0:T]
                for ch in range(KD):
                    ins = nc.scalar.activation(
                        blocks[:, ch], p_qk[:, ch * TT:(ch + 1) * TT].rearrange("p (i k) -> p i k", i=PER_TILE),
                        ACT.Identity, bias=bqk_sb[:, ch:ch + 1], scale=float(HEAD_DIM) ** -0.5)
                ins.then_inc(s_q, 1)

            def values_out(t):
                act.wait_ge(s_vp, t + 1)
                if above_zero(t):
                    act.wait_ge(s_vput, 16 * t)
                nc.scalar.activation(values[:, :], p_v, ACT.Copy).then_inc(s_values, 1)

            def load_expert(e):
                act.dma_start(w1_sb[:, bass.ds(e, 1), :, :].rearrange("p e c n -> p (e c n)"),
                              w1[bass.ds(e * P, P), :]).then_inc(s_w, 16)
                act.dma_start(w2_sb[:, bass.ds(e, 1), :, :].rearrange("p e c n -> p (e c n)"),
                              w2[bass.ds(e * P, P), :]).then_inc(s_w, 16)

            def exps(t):
                act.wait_ge(s_sub, t + 1)
                nc.scalar.activation(prob[:, :, :], prob[:, :, :], ACT.Exp).then_inc(s_exp, 1)

            def prob_out(t):
                act.wait_ge(s_pTp, t + 1)
                if above_zero(t):
                    act.wait_ge(s_o, t)
                blocks = probT[:, :, :].rearrange("p g (i s) -> p g i s", i=PER_TILE)[:, :, :, 0:T]
                nc.scalar.activation(blocks[:, 0:4], p_pT[0].rearrange("p (g i k) -> p g i k", g=4, i=PER_TILE), ACT.Copy)
                nc.scalar.activation(blocks[:, 4], p_pT[1][:, 0:TT].rearrange("p (i k) -> p i k", i=PER_TILE), ACT.Copy)
                nc.scalar.activation(blocks[0:T, 5], p_pT[1][0:T, TT:2 * TT].rearrange("p (i k) -> p i k", i=PER_TILE),
                                     ACT.Copy).then_inc(s_pT, 1)

            def xn_out(t):
                act.wait_ge(s_xnTp, t + 1)
                if above_zero(t):
                    act.wait_ge(s_affp, t)
                nc.scalar.activation(xnT[:, :, :].rearrange("p c n -> p (c n)"), p_xnT, ACT.Copy).then_inc(s_xnT, 1)

            def alpha_exp(t):
                act.wait_ge(s_amax, t + 1)
                nc.scalar.activation(aexp[:, :], amax[:, :], ACT.Exp, scale=-1.0).then_inc(s_aexp, 1)

            act.wait_ge(s_set, SETS)
            nc.scalar.activation(smax[:, 0:1], half_col[:, :], ACT.Exp)
            act.wait_ge(s_embed_w, 16 * 2)
            x_out(0)
            x_out(1)
            h_out(0)
            act.wait_ge(s_attn_w, 16 * 4)
            act.wait_ge(s_bq, 1)

            def step(q, b):
                t = 2 * q + b
                k_out(t)
                if exists(q, b, -2):
                    xn_out(t - 2)
                if exists(q, b, -1):
                    prob_out(t - 1)
                q_out(t)
                values_out(t)
                if exists(q, b, 2):
                    x_out(t + 2)
                if exists(q, b, -2):
                    alpha_exp(t - 2)
                if exists(q, b, 1):
                    h_out(t + 1)
                exps(t)
                if in_loop(t) or t < EXPERTS:
                    load_expert(t)

            step(0, 0)
            step(0, 1)
            step(1, 0)
            with act.Fori(PAIRS[0], PAIRS[1] - 1) as j:
                step(j, 1)
                step(j + 1, 0)
            for t in range(2 * PAIRS[1] - 1, TILES):
                step(t // 2, t % 2)
            prob_out(TILES - 1)
            xn_out(TILES - 2)
            alpha_exp(TILES - 2)
            xn_out(TILES - 1)
            alpha_exp(TILES - 1)

            def slot_step(j, u):
                t = RING * j + u
                act.wait_ge(s_up, KF * t + KF // 2)
                act.wait_ge(s_cur, t + 1)
                if above_zero(t - RING + 1):
                    act.wait_ge(s_down, t - RING + 1)
                for k in range(KF):
                    if k == KF // 2:
                        act.wait_ge(s_up, KF * (t + 1))
                    nc.scalar.activation(hidT[:, u, k, :], p_hidT[:, k * P:(k + 1) * P], ACT.Relu,
                                         bias=cur[:, u, 2 * KD + k:2 * KD + k + 1]).then_inc(s_relu, 1)

            for u in range(RING):
                slot_step(0, u)
            with act.Fori(*SLOT_RINGS) as j:
                for u in range(RING):
                    slot_step(j, u)
            for t in range(SLOT_RINGS[1] * RING, SLOT_TILES):
                slot_step(t // RING, t % RING)

        @block.tensor
        def _(pe):
            def x_turn(t, b):
                pe.wait_ge(s_xn, t + 1)
                if above_zero(t):
                    pe.wait_ge(s_xT, KX * t)
                for k in range(KX):
                    ins = nc.tensor.transpose(p_xT[:, k // 3, (k % 3) * TP:(k % 3 + 1) * TP],
                                              xin[:, b, k * P:(k + 1) * P], ident[0:TP, 0:TP])
                    if k % 3 == 2:
                        ins.then_inc(s_xTp, 1)

            def embed(t):
                if above_zero(t):
                    pe.wait_ge(s_z, t)
                for k in range(KX):
                    pe.wait_ge(s_xT, KX * t + k + 1)
                    ins = nc.tensor.matmul(p_z, xT[:, k, :], tokw[:, k, :], start=k == 0, stop=k == KX - 1)
                ins.then_inc(s_zp, 1)

            def h_turn(t):
                pe.wait_ge(s_hn, t + 1)
                if above_zero(t):
                    pe.wait_ge(s_hT, t)
                    pe.wait_ge(s_values, t)
                for k in range(KD):
                    ins = nc.tensor.transpose(p_hT[:, k * TT:(k + 1) * TT], hn[:, k * P:(k + 1) * P], ident[0:TT, 0:TT])
                ins.then_inc(s_hTp, 1)

            def project_qk(t):
                pe.wait_ge(s_hT, t + 1)
                if above_zero(t):
                    pe.wait_ge(s_q, t)
                    pe.wait_ge(s_k, t)
                if above_zero(t - 2):
                    pe.wait_ge(s_aff, t - 2)
                for m in range(2 * KD):
                    for k in range(KD):
                        ins = nc.tensor.matmul(p_qk[:, m * TT:(m + 1) * TT], wqk_sb[:, k, m * P:(m + 1) * P],
                                               hT[:, k, :], start=k == 0, stop=k == KD - 1)
                ins.then_inc(s_qkp, 1)

            def project_v(t):
                for k in range(KD):
                    ins = nc.tensor.matmul(p_v, hT[:, k, :], wv_sb[:, k, :], start=k == 0, stop=k == KD - 1)
                ins.then_inc(s_vp, 1)

            def scores(t, ch):
                if ch == 0:
                    pe.wait_ge(s_q, t + 1)
                    if above_zero(t):
                        pe.wait_ge(s_pT, t)
                pe.wait_ge(s_kblk, KD * t + ch + 1)
                images = LAST_IMAGES if last(t) else PER_TILE
                for i in range(images):
                    ins = nc.tensor.matmul(p_s[:, ch, :], qT[:, ch, i * TT:(i + 1) * TT],
                                           kblk[:, ch, i, :, :].rearrange("p a k -> p (a k)"),
                                           start=i == 0, stop=i == images - 1)
                if ch == KD - 1:
                    ins.then_inc(s_sp, 1)

            def prob_turn(t):
                pe.wait_ge(s_exp, t + 1)
                flat = prob[:, :, :].rearrange("p a k -> p (a k)")
                for g in range(GROUPS):
                    n = min(TT, HEADS * T - g * TT)
                    ins = nc.tensor.transpose(p_pT[g // 4][0:n, (g % 4) * TT:(g % 4 + 1) * TT],
                                              flat[:, g * TT:g * TT + n], ident[0:TT, 0:TT])
                ins.then_inc(s_pTp, 1)

            def attend(t, groups=range(GROUPS)):
                if groups[0] == 0:
                    pe.wait_ge(s_pT, t + 1)
                    pe.wait_ge(s_v, t + 1)
                    if above_zero(t):
                        pe.wait_ge(s_on, t)
                        pe.wait_ge(s_xnT, t - 1 if last(t) else t)
                for g in groups:
                    heads = min(PER_TILE, HEADS - g * PER_TILE)
                    rows_g = heads * T
                    for i in range(PER_TILE):
                        ins = nc.tensor.matmul(
                            p_o[:, g * PER_TILE * VW:(g * PER_TILE + heads) * VW],
                            probT[0:rows_g, g, i * TT:(i + 1) * TT],
                            vblk[0:rows_g, i, g * PER_TILE:g * PER_TILE + heads, :].rearrange("p a v -> p (a v)"),
                            start=i == 0, stop=i == PER_TILE - 1)
                if g == GROUPS - 1:
                    ins.then_inc(s_o, 1)

            def xn_turn(t):
                pe.wait_ge(s_x2, t + 1)
                for k in range(KD):
                    ins = nc.tensor.transpose(p_xnT[:, k * TT:(k + 1) * TT], xn[:, k * P:(k + 1) * P], ident[0:TT, 0:TT])
                ins.then_inc(s_xnTp, 1)

            def affinity(t):
                pe.wait_ge(s_xnT, t + 1)
                for k in range(KD):
                    ins = nc.tensor.matmul(p_aff, xnT[:, k, :], cent_sb[:, k, :], start=k == 0, stop=k == KD - 1)
                ins.then_inc(s_affp, 1)

            pe.wait_ge(s_set, SETS)
            pe.wait_ge(s_table, 16)
            x_turn(0, 0)
            pe.wait_ge(s_embed_w, 16 * 2)
            embed(0)
            x_turn(1, 1)
            embed(1)
            h_turn(0)
            pe.wait_ge(s_attn_w, 16 * 4)
            pe.wait_ge(s_expert_c, 16 * 2)

            def step(q, b):
                t = 2 * q + b
                project_qk(t)
                if exists(q, b, -2):
                    xn_turn(t - 2)
                if exists(q, b, -1):
                    prob_turn(t - 1)
                project_v(t)
                if last(t):
                    scores(t, 0)
                    scores(t, 1)
                    affinity(t - 2)
                    attend(t - 1)
                else:
                    if exists(q, b, -1):
                        attend(t - 1, range(GROUPS // 2))
                    scores(t, 0)
                    if exists(q, b, -2):
                        affinity(t - 2)
                    if exists(q, b, 2):
                        x_turn(t + 2, b)
                    if exists(q, b, -1):
                        attend(t - 1, range(GROUPS // 2, GROUPS))
                    scores(t, 1)
                if exists(q, b, 1):
                    h_turn(t + 1)
                if exists(q, b, 2):
                    embed(t + 2)

            step(0, 0)
            step(0, 1)
            step(1, 0)
            with pe.Fori(*PAIRS) as j:
                step(j, 1)
                step(j + 1, 0)
            for t in range(2 * PAIRS[1] + 1, TILES):
                step(t // 2, t % 2)
            prob_turn(TILES - 1)
            attend(TILES - 1)
            pe.wait_ge(s_on, TILES)
            xn_turn(TILES - 2)
            affinity(TILES - 2)
            pe.wait_ge(s_xnT, TILES - 1)
            xn_turn(TILES - 1)
            pe.wait_ge(s_aff, TILES - 1)
            affinity(TILES - 1)

            ET = EXPERTS * TILES
            hot = onehot[0:TT, :, :].rearrange("p e t -> p (e t)")
            pe.wait_ge(s_hot, 1)
            nc.tensor.matmul(p_count[0:TT, 0:ET], c("before", TT)[:, 0:TT], hot, start=True, stop=True)
            nc.tensor.matmul(p_count[:, ET:2 * ET], ones[0:TT, :], hot, start=True, stop=True).then_inc(s_count, 1)
            for t in range(TILES):
                pe.wait_ge(s_rowhot, t + 1)
                ins = nc.tensor.matmul(p_slot, row_hot[0:TT, t, :], tile_token[0:TT, t, :],
                                       start=t == 0, stop=t == TILES - 1)
            ins.then_inc(s_slotp, 1)

            def zn_turn(j, u):
                t = RING * j + u
                pe.wait_ge(s_gather[u], 16 * (j + 1))
                if above_zero(t):
                    pe.wait_ge(s_zTe, t)
                for k in range(KD):
                    ins = nc.tensor.transpose(p_zT[:, k * P:(k + 1) * P], rows[:, u, k * P:(k + 1) * P], ident)
                ins.then_inc(s_zTp, 1)

            def up(t, u):
                pe.wait_ge(s_zTe, t + 1)
                pe.wait_ge(s_w1cur, t + 1)
                for m in range(KF):
                    if m % (KF // 2) == 0 and above_zero(KF * t):
                        pe.wait_ge(s_relu, KF * (t - 1) + m + KF // 2)
                    for k in range(KD):
                        ins = nc.tensor.matmul(p_hidT[:, m * P:(m + 1) * P], w1_cur[:, u, k, m * P:(m + 1) * P],
                                               zT[:, u, k, :], start=k == 0, stop=k == KD - 1)
                    ins.then_inc(s_up, 1)

            def down(t, u, e, ks):
                final = not in_loop(t) and t == SLOT_TILES - 1
                for k in ks:
                    if k == 0 and not final and above_zero(t):
                        pe.wait_ge(s_y1, t)
                    pe.wait_ge(s_relu, KF * t + k + 1)
                    ins = nc.tensor.matmul(p_down_last if final else p_down, hidT[:, u, k, :],
                                           w2_sb[:, bass.ds(e, 1), k, :].rearrange("p e n -> p (e n)"),
                                           start=k == 0, stop=k == KF - 1)
                if k == KF - 1:
                    ins.then_inc(s_down, 1)

            pe.wait_ge(s_w, 16 * 2 * EXPERTS)
            zn_turn(0, 0)
            zn_turn(0, 1)
            up(0, 0)
            pe.wait_ge(s_expert, 1)

            def slot_step(j, u):
                t = RING * j + u
                e = pe.value_load(expert[0:1, bass.ds(t, 1)], min_val=0, max_val=EXPERTS - 1)
                if in_loop(t) or t + 1 < SLOT_TILES:
                    up(t + 1, (u + 1) % RING)
                down(t, u, e, range(KF // 2))
                if in_loop(t) or t + 2 < SLOT_TILES:
                    zn_turn(j + (u + 2) // RING, (u + 2) % RING)
                down(t, u, e, range(KF // 2, KF))

            for u in range(RING):
                slot_step(0, u)
            with pe.Fori(*SLOT_RINGS) as j:
                for u in range(RING):
                    slot_step(j, u)
            for t in range(SLOT_RINGS[1] * RING, SLOT_TILES):
                slot_step(t // RING, t % RING)

        @block.vector
        def _(dve):
            def moments(n, s_stat, s_mv, t, pieces, parts=TT):
                for i, piece in enumerate(pieces):
                    ins = nc.vector.bn_stats(stats[0:parts, n, i, :], piece)
                ins.then_inc(s_stat, 1)
                dve.wait_ge(s_stat, t + 1)
                dve.sem_inc(s_passed_dve, 1)
                nc.vector.bn_aggr(mv[0:parts, n, :],
                                  stats[0:parts, n, 0:len(pieces), :].rearrange("p a s -> p (a s)")).then_inc(s_mv, 1)

            def normalise(to, source, n, t, parts=TT):
                dve.wait_ge(s_rstd[n], t + 1)
                return nc.vector.tensor_scalar(to, source, mv[0:parts, n, 0:1], rstd[0:parts, n:n + 1],
                                               ALU.subtract, ALU.mult)

            def x_moments(q, b):
                dve.wait_ge(s_x[b], 16 * (q + 1))
                half = PATCH_DIM // 2
                moments(LN_X, s_xstat, s_xmv, 2 * q + b, [xin[:, b, 0:half], xin[:, b, half:PATCH_DIM]], TP)

            def x_norm(t, b):
                normalise(xin[:, b, :], xin[:, b, :], LN_X, t, TP).then_inc(s_xn, 1)

            def z_moments(t):
                dve.wait_ge(s_zp, t + 1)
                nc.vector.tensor_tensor(z[:, :], p_z, tok_row[:, :], ALU.add).then_inc(s_z, 1)
                dve.wait_ge(s_z, t + 1)
                moments(LN_Z, s_zstat, s_zmv, t, [z[:, :]])

            def h_moments(t):
                normalise(z[:, :], z[:, :], LN_Z, t).then_inc(s_zn, 1)
                dve.wait_ge(s_zn, t + 1)
                nc.vector.tensor_tensor(z[:, :], z[:, :], gain[:, :], ALU.mult).then_inc(s_zg, 1)
                dve.wait_ge(s_zg, t + 1)
                if above_zero(t):
                    dve.wait_ge(s_hb, t)
                nc.vector.tensor_tensor(h[:, :], z[:, :], shift[:, :], ALU.add).then_inc(s_h, 1)
                dve.wait_ge(s_h, t + 1)
                moments(LN_H, s_hstat, s_hmv, t, [h[:, :]])

            def h_norm(t):
                if above_zero(t):
                    dve.wait_ge(s_hTp, t)
                normalise(hn[:, :], h[:, :], LN_H, t).then_inc(s_hn, 1)

            def softmax_in(t):
                dve.wait_ge(s_sp, t + 1)
                if above_zero(t):
                    dve.wait_ge(s_pTp, t)
                nc.vector.tensor_tensor(
                    prob[:, :, :].rearrange("p (c a) k -> p c a k", c=KD), p_s.rearrange("p c (a k) -> p c a k", a=HC),
                    c("causal", TT).unsqueeze(1).unsqueeze(1).to_broadcast([TT, KD, HC, T]), ALU.add).then_inc(s_sm, 1)
                dve.wait_ge(s_sm, t + 1)
                nc.vector.tensor_reduce(smax[:, :], prob[:, :, :], AX.X, ALU.max).then_inc(s_smax, 1)
                dve.wait_ge(s_smax, t + 1)
                nc.vector.tensor_tensor(prob[:, :, :], prob[:, :, :],
                                        smax[:, :].unsqueeze(2).to_broadcast([TT, HEADS, T]),
                                        ALU.subtract).then_inc(s_sub, 1)

            def h1_moments(t, b):
                dve.wait_ge(s_o, t + 1)
                o = p_o.rearrange("p (a v) -> p a v", a=HEADS)
                nc.vector.reciprocal(srec[:, :], o[:, :, HEAD_DIM]).then_inc(s_rec, 1)
                dve.wait_ge(s_rec, t + 1)
                if above_zero(t):
                    dve.wait_ge(s_base, t)
                nc.vector.tensor_tensor(h1[:, :].rearrange("p (a d) -> p a d", a=HEADS), o[:, :, 0:HEAD_DIM],
                                        srec[:, :].unsqueeze(2).to_broadcast([TT, HEADS, HEAD_DIM]),
                                        ALU.mult).then_inc(s_on, 1)
                dve.wait_ge(s_on, t + 1)
                dve.wait_ge(s_hb, t + 1)
                nc.vector.tensor_tensor(h1[:, :], h1[:, :], hb[:, b, :], ALU.add).then_inc(s_h1, 1)
                dve.wait_ge(s_h1, t + 1)
                moments(LN_H1, s_h1stat, s_h1mv, t, [h1[:, :]])

            def xn_moments(t):
                if above_zero(t):
                    dve.wait_ge(s_xnTp, t)
                if above_zero(t):
                    dve.wait_ge(s_base, t)
                normalise(xn[:, :], h1[:, :], LN_H1, t).then_inc(s_x2, 1)
                dve.wait_ge(s_x2, t + 1)
                moments(LN_XN, s_x2stat, s_x2mv, t, [xn[:, :]])

            def zn_row(q, b):
                if above_zero(q):
                    dve.wait_ge(s_stored[b], 16 * q)
                normalise(rowbuf[:, b, 0:D], xn[:, :], LN_XN, 2 * q + b).then_inc(s_row, 1)

            def keep_affinity(t):
                dve.wait_ge(s_affp, t + 1)
                nc.vector.tensor_reduce(amax[:, :], p_aff, AX.X, ALU.max).then_inc(s_amax, 1)
                nc.vector.tensor_copy(aff_all[0:TT, bass.ds(t, 1), :].rearrange("p t e -> p (t e)"), p_aff)\
                    .then_inc(s_aff, 1)

            def alpha(t, b):
                dve.wait_ge(s_aexp, t + 1)
                nc.vector.tensor_scalar(ainc[:, :], aexp[:, :], 1.0, None, ALU.add).then_inc(s_ainc, 1)
                dve.wait_ge(s_ainc, t + 1)
                nc.vector.reciprocal(rowbuf[:, b, 2 * D:2 * D + 1], ainc[:, :]).then_inc(s_alpha, 1)

            nc.vector.memset(ones[:], 1.0).then_inc(s_set, 1)
            nc.vector.memset(rowbuf[:, :, 2 * D:ROW], 0.0).then_inc(s_set, 1)
            dve.wait_ge(s_table, 16)
            for i in range(PER_TILE):
                nc.vector.tensor_copy(vblk[:, i, :, HEAD_DIM], c("head_in_stack", TT)).then_inc(s_set, 1)

            dve.wait_ge(s_set, SETS)
            x_moments(0, 0)
            x_norm(0, 0)
            x_moments(0, 1)
            x_norm(1, 1)
            dve.wait_ge(s_rows, 16 * 4)
            nc.vector.tensor_tensor(shift[:, :], shift[:, :], shift2[:, :], ALU.add).then_inc(s_shift, 1)
            dve.wait_ge(s_attn_w, 16 * 4)
            nc.vector.tensor_scalar(bqk_sb[:, 0:KD], bqk_sb[:, 0:KD], float(HEAD_DIM) ** -0.5, None, ALU.mult)\
                .then_inc(s_bq, 1)
            dve.wait_ge(s_shift, 1)
            z_moments(0)
            h_moments(0)
            h_norm(0)
            z_moments(1)
            dve.wait_ge(s_expert_c, 16 * 2)

            def step(q, b):
                t = 2 * q + b
                if exists(q, b, 2):
                    x_moments(*at(q, b, 2))
                if exists(q, b, 1):
                    h_moments(t + 1)
                if exists(q, b, 2):
                    x_norm(t + 2, b)
                if exists(q, b, 1):
                    h_norm(t + 1)
                if exists(q, b, -2):
                    keep_affinity(t - 2)
                if last(t):
                    softmax_in(t)
                if exists(q, b, -1):
                    h1_moments(t - 1, 1 - b)
                if not last(t):
                    softmax_in(t)
                if exists(q, b, -1):
                    xn_moments(t - 1)
                if exists(q, b, -2):
                    alpha(t - 2, b)
                if exists(q, b, 2):
                    z_moments(t + 2)
                if exists(q, b, -1):
                    zn_row(*at(q, b, -1))

            step(0, 0)
            step(0, 1)
            step(1, 0)
            with dve.Fori(*PAIRS) as j:
                step(j, 1)
                step(j + 1, 0)
            for t in range(2 * PAIRS[1] + 1, TILES):
                step(t // 2, t % 2)
            end = TILES - 1
            h1_moments(end, end % 2)
            keep_affinity(end - 1)
            xn_moments(end)
            alpha(end - 1, 1 - end % 2)
            zn_row(end // 2, end % 2)
            keep_affinity(end)

            steps = [0]

            def beside(ins):
                steps[0] += 1
                ins.then_inc(r_dve, 1)

            def then(ins):
                beside(ins)
                dve.wait_ge(r_dve, steps[0])

            def wide(ap, shape, *axes):
                for a in axes:
                    ap = ap.unsqueeze(a)
                return ap.to_broadcast(shape)

            ET = EXPERTS * TILES
            aff = aff_all[0:TT, :, :]
            te = [TT, TILES, EXPERTS]
            et = [TT, EXPERTS, TILES]
            dve.wait_ge(s_aff, TILES)
            then(nc.vector.tensor_reduce(r_max[0:TT, :], aff, AX.X, ALU.max))
            then(nc.vector.tensor_tensor(r_val[0:TT], aff, wide(r_max[0:TT, :], te, 2), ALU.is_ge))
            then(nc.vector.tensor_tensor(r_val[0:TT], r_val[0:TT], wide(c("rank", TT), te, 1), ALU.mult))
            then(nc.vector.tensor_reduce(r_first[0:TT, :], r_val[0:TT], AX.X, ALU.max))
            then(nc.vector.tensor_tensor(r_val[0:TT], r_val[0:TT], wide(r_first[0:TT, :], te, 2), ALU.is_equal))
            nc.vector.tensor_tensor(onehot[0:TT].rearrange("p e t -> p t e"), r_val[0:TT],
                                    wide(c("live", TT), te, 2), ALU.mult).then_inc(s_hot, 1)
            alpha(end, end % 2)
            dve.wait_ge(s_count, 1)
            then(nc.vector.tensor_copy(tot[:, :, :].rearrange("p e t -> p (e t)"), p_count[:, ET:2 * ET]))
            then(nc.vector.tensor_tensor_scan(through[:, :, :].rearrange("p e t -> p (e t)"), c("restart"),
                                              tot[:, :, :].rearrange("p e t -> p (e t)"), 0.0, ALU.mult, ALU.add))
            shape = [P, EXPERTS, TOKENS // P + 1]
            beside(nc.vector.tensor_tensor(r_cmp[:, :, :], through[:, :, TILES - 1].unsqueeze(2).to_broadcast(shape),
                                           wide(c("gt_slots"), shape, 1), ALU.is_gt))
            then(nc.vector.tensor_tensor(place[0:TT], through[0:TT], tot[0:TT], ALU.subtract))
            beside(nc.vector.tensor_reduce(n_tiles[:, :], r_cmp[:, :, :], AX.X, ALU.add))
            then(nc.vector.tensor_tensor(place[0:TT], place[0:TT],
                                         p_count[0:TT, 0:ET].rearrange("p (e t) -> p e t", e=EXPERTS), ALU.add))
            then(nc.vector.tensor_tensor_scan(tile_end[:, :], ones[:, 0:EXPERTS], n_tiles[:, :], 0.0,
                                              ALU.mult, ALU.add))
            then(nc.vector.tensor_tensor(tile_start[:, :], tile_end[:, :], n_tiles[:, :], ALU.subtract))
            then(nc.vector.scalar_tensor_tensor(place[0:TT], wide(tile_start[0:TT, :], et, 2), float(P), place[0:TT],
                                                ALU.mult, ALU.add))
            then(nc.vector.tensor_tensor(place[0:TT], place[0:TT], onehot[0:TT], ALU.mult))
            then(nc.vector.tensor_reduce(pos[0:TT, :], place[0:TT].rearrange("p e t -> p t e"), AX.X, ALU.add))
            shape = [TT, TILES, SLOT_TILES - 1]
            then(nc.vector.tensor_tensor(r_ge[0:TT], wide(pos[0:TT, :], shape, 2), wide(c("ge_slots", TT), shape, 1),
                                         ALU.is_ge))
            then(nc.vector.tensor_reduce(slot_tile[0:TT, :], r_ge[0:TT], AX.X, ALU.add))
            beside(nc.vector.scalar_tensor_tensor(slot_row[0:TT, :], slot_tile[0:TT, :], -float(P), pos[0:TT, :],
                                                  ALU.mult, ALU.add))
            shape = [TT, TILES, SLOT_TILES]
            then(nc.vector.tensor_tensor(tile_hot[0:TT], wide(slot_tile[0:TT, :], shape, 2),
                                         wide(c("tile_no", TT), shape, 1), ALU.is_equal))
            beside(nc.vector.tensor_tensor(tile_token[0:TT], tile_hot[0:TT], wide(c("token", TT), shape, 2), ALU.mult))
            for t in range(TILES):
                nc.vector.tensor_scalar(row_hot[0:TT, t, :], c("iota", TT), slot_row[0:TT, t:t + 1], None,
                                        ALU.is_equal).then_inc(s_rowhot, 1)
            dve.wait_ge(s_slotp, 1)
            nc.vector.tensor_scalar(gather_all[:, :], p_slot, 1.0, 0.0, ALU.subtract, ALU.max).then_inc(s_route, 1)
            then(nc.vector.tensor_scalar(empty[:, :], p_slot, 0.5, NO_TOKEN, ALU.is_lt, ALU.mult))
            beside(nc.vector.scalar_tensor_tensor(scatter_all[:, :], p_slot, 1.0, empty[:, :], ALU.subtract, ALU.add))
            shape = [P, SLOT_TILES, EXPERTS]
            then(nc.vector.tensor_tensor(e_cmp[:, :, :], wide(c("tile_no"), shape, 2), wide(tile_end[:, :], shape, 1),
                                         ALU.is_ge))
            then(nc.vector.tensor_reduce(e_sum[:, :], e_cmp[:, :, :], AX.X, ALU.add))
            nc.vector.tensor_scalar(expert[:, :], e_sum[:, :], EXPERTS - 1.0, None, ALU.min).then_inc(s_expert, 1)
            dve.wait_ge(s_expert, 1)

            def columns(j, u):
                t = RING * j + u
                e = dve.value_load(expert[0:1, bass.ds(t, 1)], min_val=0, max_val=EXPERTS - 1)
                if above_zero(t - RING + 1):
                    dve.wait_ge(s_relu, KF * (t - RING + 1))
                nc.vector.tensor_copy(cur[:, u, :], cols_sb[:, bass.ds(e, 1), :].rearrange("p e n -> p (e n)"))\
                    .then_inc(s_cur, 1)
                nc.vector.tensor_copy(b2_cur[:, u, :], b2_sb[:, bass.ds(e, 1), :].rearrange("p e n -> p (e n)"))\
                    .then_inc(s_b2cur, 1)
                nc.vector.tensor_copy(w1_cur[:, u, :, :].rearrange("p c n -> p (c n)"),
                                      w1_sb[:, bass.ds(e, 1), :, :].rearrange("p e c n -> p (e c n)"))\
                    .then_inc(s_w1cur, 1)

            def z_out(t, u):
                dve.wait_ge(s_zTp, t + 1)
                dve.wait_ge(s_cur, t + 1)
                if above_zero(t - RING + 1):
                    dve.wait_ge(s_up, KF * (t - RING + 1))
                for k in range(KD):
                    ins = nc.vector.tensor_scalar(zT[:, u, k, :], p_zT[:, k * P:(k + 1) * P], cur[:, u, k:k + 1],
                                                  cur[:, u, KD + k:KD + k + 1], ALU.mult, ALU.add)
                ins.then_inc(s_zTe, 1)

            def finish(j, u):
                t = RING * j + u
                dve.wait_ge(s_down, t + 1)
                dve.wait_ge(s_b2cur, t + 1)
                if above_zero(t):
                    dve.wait_ge(s_y, t)
                summed = p_down_last if not in_loop(t) and t == SLOT_TILES - 1 else p_down
                nc.vector.tensor_tensor(y1[:, :], summed, b2_cur[:, u, :], ALU.add).then_inc(s_y1, 1)
                dve.wait_ge(s_y1, t + 1)
                dve.wait_ge(s_gather[u], 16 * (j + 1))
                if above_zero(16 * j):
                    dve.wait_ge(s_scatter[u], 16 * j)
                nc.vector.scalar_tensor_tensor(yout[:, u, :], y1[:, :], rows[:, u, 2 * D:2 * D + 1],
                                               rows[:, u, D:2 * D], ALU.mult, ALU.add).then_inc(s_y, 1)

            dve.wait_ge(s_w, 16 * 2 * EXPERTS)
            dve.wait_ge(s_b2, 16)
            columns(0, 0)
            z_out(0, 0)
            columns(0, 1)
            z_out(1, 1)
            columns(0, 2)

            def slot_step(j, u):
                t = RING * j + u
                if in_loop(t) or t + 2 < SLOT_TILES:
                    z_out(t + 2, (u + 2) % RING)
                finish(j, u)
                if in_loop(t) or t + RING < SLOT_TILES:
                    columns(j + 1, u)

            for u in range(RING):
                slot_step(0, u)
            with dve.Fori(*SLOT_RINGS) as j:
                for u in range(RING):
                    slot_step(j, u)
            for t in range(SLOT_RINGS[1] * RING, SLOT_TILES):
                slot_step(t // RING, t % RING)


def _table():
    t = np.zeros((P, TABLE), np.float32)
    p = np.arange(P)[:, None]

    def put(name, value):
        a, w = COLS[name]
        t[:, a:a + w] = value

    put("ident", p == np.arange(P))
    put("before", p < np.arange(P))
    put("iota", np.arange(P))
    put("head_of_row", p // HEAD_DIM == np.arange(HC))
    put("head_in_stack", p // T == np.arange(HEADS) % PER_TILE)
    put("causal", np.where(np.arange(T) <= p % T, 0.0, MASKED))
    token = np.arange(TILES) * TT + p
    put("token", (token + 1) * (token < TOKENS))
    put("live", token < TOKENS)
    put("ge_slots", P * np.arange(1, SLOT_TILES))
    put("gt_slots", P * np.arange(TOKENS // P + 1))
    put("tile_no", np.arange(SLOT_TILES))
    put("rank", EXPERTS - np.arange(EXPERTS))
    put("restart", np.tile(np.arange(TILES) > 0, EXPERTS))
    return t


def _positions():
    ys, xs = np.meshgrid(np.arange(GRID), np.arange(GRID), indexing="ij")
    omega = np.arange(D // 4, dtype=np.float32) / np.float32(D // 4 - 1)
    omega = (np.float32(1.0) / np.float32(TEMPERATURE) ** omega).astype(np.float32)
    ys = ys.reshape(-1)[:, None].astype(np.float32) * omega
    xs = xs.reshape(-1)[:, None].astype(np.float32) * omega
    return np.concatenate([np.sin(xs), np.cos(xs), np.sin(ys), np.cos(ys)], axis=1).astype(np.float32)


def _chunks(a):
    return np.ascontiguousarray(a.reshape(-1, P, a.shape[-1]).transpose(1, 0, 2).reshape(P, -1))


def kernel(x, cls_tok, L0_tok_cls_token, L0_tok_cls_pos_embedding, L0_tok_ln1_g, L0_tok_ln1_b, L0_tok_W,
           L0_tok_bias, L0_tok_ln2_g, L0_tok_ln2_b, L0_attn_W, L0_attn_b, L0_ffn_centroids, L0_ffn_ln_g,
           L0_ffn_ln_b, L0_ffn_w1, L0_ffn_b1, L0_ffn_w2, L0_ffn_b2):
    import concourse.bacc as bacc
    from concourse.bass_utils import run_bass_kernel_spmd

    x = np.asarray(x).reshape(IMAGES, CHANNELS, GRID, PATCH, GRID, PATCH)
    patches = x.transpose(0, 2, 4, 3, 5, 1).reshape(IMAGES * PATCHES, PATCH_DIM)

    def row(a):
        return np.asarray(a).reshape(1, -1)

    def image_rows(first, second, patch):
        patch = np.broadcast_to(patch, (PATCHES, D))
        return np.tile(np.concatenate([first, second, patch]), (PER_TILE, 1))

    none = np.zeros((1, D), np.float32)
    attn_w = np.asarray(L0_attn_W)
    attn_b = np.asarray(L0_attn_b)
    cols = np.concatenate([np.asarray(a).reshape(EXPERTS, -1, P) for a in (L0_ffn_ln_g, L0_ffn_ln_b, L0_ffn_b1)],
                          axis=1)
    w1 = np.asarray(L0_ffn_w1).transpose(0, 2, 1).reshape(EXPERTS, KD, P, HIDDEN).transpose(0, 2, 1, 3)
    w2 = np.asarray(L0_ffn_w2).transpose(0, 2, 1).reshape(EXPERTS, KF, P, D).transpose(0, 2, 1, 3)
    inputs = {
        "x": patches,
        "tok_add": image_rows(row(cls_tok), row(L0_tok_cls_token), row(L0_tok_ln2_b)),
        "tok_add2": image_rows(none, row(L0_tok_cls_pos_embedding), _positions()),
        "tok_gain": image_rows(none, none, row(L0_tok_ln2_g)),
        "ln1_gb": np.concatenate([np.asarray(L0_tok_ln1_g), np.asarray(L0_tok_ln1_b)]).reshape(2 * KX, P).T,
        "tok_w": _chunks(np.asarray(L0_tok_W)),
        "tok_bias": np.asarray(L0_tok_bias).reshape(D),
        "wqk": _chunks(attn_w[0:2 * D].T),
        "wv": _chunks(attn_w[2 * D:].T),
        "bqk": attn_b[0:2 * D].reshape(2 * KD, P).T,
        "bv": attn_b[2 * D:],
        "centroids": _chunks(np.asarray(L0_ffn_centroids).T),
        "expert_cols": cols.transpose(2, 0, 1).reshape(P, -1),
        "expert_b2": np.asarray(L0_ffn_b2).reshape(-1),
        "w1": w1.reshape(EXPERTS * P, -1),
        "w2": w2.reshape(EXPERTS * P, -1),
        "table": _table(),
    }
    nc = bacc.Bacc("TRN2", target_bir_lowering=False, num_devices=1)
    arrays, aps = {}, {}
    for name, a in inputs.items():
        a = np.ascontiguousarray(a)
        arrays[f"in_{name}"] = a
        aps[name] = nc.dram_tensor(f"in_{name}", a.shape, mybir.dt.from_np(a.dtype), kind="ExternalInput").ap()
    out = nc.dram_tensor("out", (TOKENS, D), F32, kind="ExternalOutput").ap()
    attention_tower(nc, out=out, **aps)
    r = run_bass_kernel_spmd(nc, [arrays], core_ids=[0])
    return r.results[0]["out"].reshape(IMAGES, T, D)
```
